# Optimizing a Trainium2 kernel written in Bass

```python
import numpy as np
import jax
import jax.numpy as jnp

def _softmax(x, axis=-1):
    return jax.nn.softmax(x, axis=axis)

def _gelu(x):
    return jax.nn.gelu(x, approximate=True)

def _silu(x):
    return jax.nn.silu(x)

def _sigmoid(x):
    return jax.nn.sigmoid(x)

def _layernorm(x, axis=-1, eps=1e-05):
    m = jnp.mean(x, axis=axis, keepdims=True)
    v = jnp.var(x, axis=axis, keepdims=True)
    return (x - m) / jnp.sqrt(v + eps)

def _scatter_add(tgt, idx, src, axis=0):
    return tgt.at[idx].add(src)

def _segment_sum(src, seg, n):
    return jax.ops.segment_sum(src, seg, n)
kernel_name = 'mk_xattn_ffn_d1_seqx_r4_e438a9'

def setup_inputs(seed: int=0):
    np.random.seed(seed)
    _w = jnp.asarray

    def _rec_inputs():
        import jax
        import jax.numpy as jnp
        _rk = jax.random.key(seed)
        x = -1.394e-06 + 0.9999 * jax.random.normal(jax.random.fold_in(_rk, 1), (8, 512, 256), jnp.float32)
        _lenS = 512 - jax.random.randint(jax.random.fold_in(_rk, 7), (8,), 0, max(1, 512 // 4) + 1, jnp.int32)
        _lenS2 = 512 - jax.random.randint(jax.random.fold_in(_rk, 8), (8,), 0, max(1, 512 // 4) + 1, jnp.int32)
        _ctx_1024P = jax.random.normal(jax.random.fold_in(_rk, 11), (8, 16, 256), jnp.float32)
        _ctx_1024c = jax.random.dirichlet(jax.random.fold_in(_rk, 511), 0.3 * jnp.ones((16,), jnp.float32), (8, 512))
        _ctx_1024t = jnp.einsum('bsk,bkd->bsd', _ctx_1024c, _ctx_1024P)
        _ctx_1024t = _ctx_1024t * jax.lax.rsqrt(jnp.mean(jnp.square(_ctx_1024t)) + 1e-12) * 0.953939
        ctx_1024 = -0.000292821 + 1.00034 * (_ctx_1024t + 0.3 * jax.random.normal(jax.random.fold_in(_rk, 611), (8, 512, 256), jnp.float32))
        return (x, ctx_1024)
    x, ctx_1024 = _rec_inputs()

    def _L0_xattn_setup():
        import jax, jax.numpy as jnp
        import numpy as np
        NUM_HEADS = 16
        D_MODEL = 256
        LN_EPS = 1e-05
        key = jax.random.key(seed)
        ks = jax.random.split(key, 10)
        B, S, D = (2, 512, D_MODEL)
        s = 1.0 / np.sqrt(D)
        return {'encoded': jax.random.normal(ks[0], (B, S, D), jnp.float32), 'decoded': jax.random.normal(ks[1], (B, S, D), jnp.float32), 'Wq': jax.random.normal(ks[2], (D, D), jnp.float32) * s, 'bq': jax.random.normal(ks[3], (D,), jnp.float32) * s, 'Wk': jax.random.normal(ks[4], (D, D), jnp.float32) * s, 'bk': jax.random.normal(ks[5], (D,), jnp.float32) * s, 'Wv': jax.random.normal(ks[6], (D, D), jnp.float32) * s, 'bv': jax.random.normal(ks[7], (D,), jnp.float32) * s, 'gamma': jnp.ones((D,), jnp.float32), 'beta': jnp.zeros((D,), jnp.float32)}
    _L0_xattn_all = _L0_xattn_setup()
    _L0_xattn_in = {k: v for k, v in _L0_xattn_all.items() if k in ('Wq', 'bq', 'Wk', 'bk', 'Wv', 'bv', 'gamma', 'beta')}
    del _L0_xattn_all

    def _L0_ffn_setup():
        import jax, jax.numpy as jnp
        import numpy as np
        B, S, H, E = (2, 2048, 256, 8)
        SCALE = 0.5
        key = jax.random.key(seed)
        k1, k2 = jax.random.split(key)
        x = jax.random.normal(k1, (B, S, H), dtype=jnp.float32)
        gate_w = jax.random.normal(k2, (E, H), dtype=jnp.float32) * 0.02
        coeff = SCALE * (1.0 + 0.05 * jnp.arange(E, dtype=jnp.float32))
        expert_w = coeff[:, None, None] * jnp.eye(H, dtype=jnp.float32)
        return {'x': x, 'gate_w': gate_w, 'expert_w': expert_w}
    _L0_ffn_all = _L0_ffn_setup()
    _L0_ffn_in = {k: v for k, v in _L0_ffn_all.items() if k in ('gate_w', 'expert_w')}
    del _L0_ffn_all
    return {'x': x, 'ctx_1024': ctx_1024, 'L0_xattn_Wq': _L0_xattn_in['Wq'], 'L0_xattn_bq': _L0_xattn_in['bq'], 'L0_xattn_Wk': _L0_xattn_in['Wk'], 'L0_xattn_bk': _L0_xattn_in['bk'], 'L0_xattn_Wv': _L0_xattn_in['Wv'], 'L0_xattn_bv': _L0_xattn_in['bv'], 'L0_xattn_gamma': _L0_xattn_in['gamma'], 'L0_xattn_beta': _L0_xattn_in['beta'], 'L0_ffn_gate_w': _L0_ffn_in['gate_w'], 'L0_ffn_expert_w': _L0_ffn_in['expert_w']}

def reference(x, ctx_1024, L0_xattn_Wq, L0_xattn_bq, L0_xattn_Wk, L0_xattn_bk, L0_xattn_Wv, L0_xattn_bv, L0_xattn_gamma, L0_xattn_beta, L0_ffn_gate_w, L0_ffn_expert_w):
    import jax
    import jax.numpy as jnp

    def _L0_xattn_ref(encoded, decoded, Wq, bq, Wk, bk, Wv, bv, gamma, beta):
        import jax, jax.numpy as jnp
        import numpy as np
        NUM_HEADS = 16
        D_MODEL = 256
        LN_EPS = 1e-05
        B, Sq, D = decoded.shape
        H = NUM_HEADS
        dh = D // H
        q = decoded @ Wq.T + bq
        k = encoded @ Wk.T + bk
        v = encoded @ Wv.T + bv
        q = q.reshape(B, Sq, H, dh).transpose(0, 2, 1, 3)
        k = k.reshape(B, -1, H, dh).transpose(0, 2, 1, 3)
        v = v.reshape(B, -1, H, dh).transpose(0, 2, 1, 3)
        qk = jnp.einsum('bhqd,bhkd->bhqk', q, k)
        qk = jnp.where(jnp.isnan(qk), -jnp.inf, qk)
        attn = jax.nn.softmax(qk, axis=-1)
        attn = jnp.where(jnp.isnan(attn), 0.0, attn)
        v = jnp.where(jnp.isnan(v), 0.0, v)
        z = jnp.einsum('bhqk,bhkd->bhqd', attn, v)
        z = z.reshape(B, Sq, D)
        x = z + decoded
        mu = jnp.mean(x, axis=-1, keepdims=True)
        var = jnp.var(x, axis=-1, keepdims=True)
        return (x - mu) * jax.lax.rsqrt(var + LN_EPS) * gamma + beta

    def _L0_ffn_ref(x, gate_w, expert_w):
        import jax, jax.numpy as jnp
        import numpy as np
        B, S, H, E = (2, 2048, 256, 8)
        SCALE = 0.5
        scores = jnp.einsum('bsh,eh->bse', x, gate_w)
        chosen = jnp.argmax(scores, axis=-1)
        onehot = jax.nn.one_hot(chosen, gate_w.shape[0], dtype=x.dtype)
        expert_out = jnp.einsum('bsh,efh->bsef', x, expert_w)
        return x + jnp.einsum('bsef,bse->bsf', expert_out, onehot)
    x = x + _L0_xattn_ref(ctx_1024, _layernorm(x, axis=-1), L0_xattn_Wq, L0_xattn_bq, L0_xattn_Wk, L0_xattn_bk, L0_xattn_Wv, L0_xattn_bv, L0_xattn_gamma, L0_xattn_beta)
    x = x + _L0_ffn_ref(_layernorm(x, axis=-1), L0_ffn_gate_w, L0_ffn_expert_w)
    return x

_drawn_inputs = setup_inputs


def setup_inputs(seed=0):
    import zlib

    import numpy as np

    out = dict(_drawn_inputs(seed))
    spreads = {'L0_xattn_gamma': (1.0, 0.2), 'L0_xattn_beta': (0.0, 0.1)}
    factors = {}
    for name, (base, spread) in spreads.items():
        noise = np.random.default_rng([zlib.crc32(name.encode()), seed]).standard_normal(out[name].shape)
        drawn = base * np.exp(spread * noise) if base else spread * noise
        out[name] = jnp.asarray(drawn.astype(out[name].dtype))
    for name, factor in factors.items():
        out[name] = (out[name] * factor).astype(out[name].dtype)
    return out
```

```python
from contextlib import ExitStack

import concourse.bass as bass
from concourse import mybir

P = 128
F32 = mybir.dt.float32
BF16 = mybir.dt.bfloat16
ALU = mybir.AluOpType
ACT = mybir.ActivationFunctionType
AX_X = mybir.AxisListType.X

H = 16
EPS = 1e-5
Q_BLOCKS = (0, 0, 1, 1, 0, 2)
K_BLOCKS = (0, 1, 0, 1, 2, 0)
NBLK = len(Q_BLOCKS)


def xattn_ffn_kernel(nc: bass.Bass, x, ctxT, WqT, bq, WkT, bk, WvT, bv, gamma, beta, gateT, expertT, identity_in, out):
    B, S, D = x.shape
    DH = D // H
    TT = S // P
    KC = D // P
    E = gateT.shape[1]
    HG = 4
    NG = H // HG
    GALL = B * NG
    HH = H // KC
    ROWS = NBLK * DH
    SROWS = ROWS + 3
    NT = B * TT
    LOADS = 16

    with ExitStack() as ctx:
        def sb(name, shape, dt=F32):
            return ctx.enter_context(nc.sbuf_tensor(name, shape, dt))

        def sem(name):
            return ctx.enter_context(nc.semaphore(name))

        identity = sb("identity", [P, P])
        wq = sb("wq", [P, KC, D])
        wk = sb("wk", [P, KC, D])
        wv = sb("wv", [P, KC, D])
        bias_q = sb("bias_q", [P, KC])
        bias_k = sb("bias_k", [P, KC])
        bias_v = sb("bias_v", [P, D])
        gamma_bc = sb("gamma_bc", [P, D])
        beta_bc = sb("beta_bc", [P, D])
        tiny = sb("tiny", [P, 1])
        zeros = sb("zeros", [HG * TT, P])
        gate = sb("gate", [P, KC, E])
        eps = sb("eps", [P, 1])
        rank_weight = sb("rank_weight", [P, E])
        normed = sb("normed", [P, NT, D])
        v_all = sb("v_all", [P, B, TT, D])
        work = sb("work", [P, 16384])
        q_op = sb("q_op", [P, H, S], BF16)
        k_op = sb("k_op", [P, H, S], BF16)
        v_aug = sb("v_aug", [P, 2, TT, HG, 2 * DH])
        zt = sb("zt", [P, 2, DH, 2 * DH])
        z_sb = sb("z_sb", [P, 2, DH, DH])
        row_max = sb("row_max", [P, 2, HG * TT])
        recip = sb("recip", [P, 2, DH])
        shift_parts = sb("shift_parts", [HG * TT, 2, 3, P], BF16)
        shift_rest = sb("shift_rest", [HG * TT, 2, P])
        bn = sb("bn", [P, 2, TT, 6])
        mv = sb("mv", [P, 2, TT, 2])
        std = sb("std", [P, 2, TT])
        rstd = sb("rstd", [P, 2, TT])
        ps = ctx.enter_context(nc.psum_tensor("ps", [P, 8, 512], F32))

        off = [0]

        def take(n):
            off[0] += n
            return work[:, off[0] - n:off[0]]

        x_in = [take(TT * D).rearrange("p (t d) -> p t d", t=TT) for _ in range(2)]
        xn = [take(TT * D).rearrange("p (t d) -> p t d", t=TT) for _ in range(2)]
        xnT = [take(KC * S).rearrange("p (c s) -> p c s", c=KC) for _ in range(2)]
        ctx_in = [take(KC * S).rearrange("p (c s) -> p c s", c=KC) for _ in range(2)]
        parts = [take(2 * 3 * KC * S // 2).bitcast(BF16).rearrange("p (q a m s) -> p q a m s", q=2, a=3, m=KC)
                 for _ in range(2)]
        rest = take(2 * KC * S).rearrange("p (q m s) -> p q m s", q=2, m=KC)
        probs = work[:, :].rearrange("p (g h k q) -> p g h k q", g=2, h=HG, k=TT)
        experts = v_all[:, :, :, :].rearrange("p b t d -> p (b t d)")[:, 0:KC * E * D].rearrange("p (c n) -> p c n", c=KC)
        x_res = [work[:, i * D:(i + 1) * D] for i in (0, 1)]
        u = [work[:, i * D:(i + 1) * D] for i in (2, 3)]
        x1 = [work[:, i * D:(i + 1) * D] for i in (4, 5)]
        xf = [work[:, i * D:(i + 1) * D] for i in (6, 7)]
        xfT = [work[:, i * D:(i + 1) * D].rearrange("p (c s) -> p c s", c=KC) for i in (8, 9)]
        acc = [work[:, i * D:(i + 1) * D] for i in (10, 11)]
        smalls = work[:, 12 * D:13 * D]

        op_scr = nc.dram_tensor("op_scr", [B, 2, KC, ROWS, HH * S], BF16, kind="Internal").ap()
        sh_scr = nc.dram_tensor("sh_scr", [2, 3, HG * TT, P], BF16, kind="Internal").ap()

        x_b = x.rearrange("b (t p) d -> b p t d", p=P)
        ctxT_b = ctxT.rearrange("b (c p) s -> b p c s", p=P)
        x_t = x.rearrange("b (t p) d -> (b t) p d", p=P)
        out_t = out.rearrange("b (t p) d -> (b t) p d", p=P)

        consts_in = sem("consts_in")
        consts_set = sem("consts_set")
        batch_in = [sem(f"batch_in{j}") for j in range(2)]
        var_done = sem("var_done")
        stats_step = sem("stats_step")
        std_done = sem("std_done")
        rstd_done = sem("rstd_done")
        xn_done = sem("xn_done")
        xn_kept = sem("xn_kept")
        xT_ready = sem("xT_ready")
        xnT_done = sem("xnT_done")
        k_ready = sem("k_ready")
        v_ready = sem("v_ready")
        q_ready = sem("q_ready")
        hi_done = [sem("hi_q"), sem("hi_k")]
        rest_done = [sem("rest_q"), sem("rest_k")]
        mid_done = [sem("mid_q"), sem("mid_k")]
        lo_done = [sem("lo_q"), sem("lo_k")]
        v_done = sem("v_done")
        op_stored = [sem(f"op_stored{j}") for j in range(2)]
        STORES = 2 * NBLK * LOADS
        op_loaded = [sem(f"op_loaded{g}") for g in range(NG)]
        scores_ready = sem("scores_ready")
        max_done = sem("max_done")
        maxT_ready = sem("maxT_ready")
        sh_hi = sem("sh_hi")
        sh_rest = sem("sh_rest")
        sh_mid = sem("sh_mid")
        sh_lo = sem("sh_lo")
        sh_stored = sem("sh_stored")
        sh_loaded = [sem(f"sh_loaded{j}") for j in range(2)]
        st_ready = sem("st_ready")
        exp_done = sem("exp_done")
        v_aug_done = sem("v_aug_done")
        pv_done = sem("pv_done")
        zt_done = sem("zt_done")
        recip_done = sem("recip_done")
        z_done = sem("z_done")
        y_done = sem("y_done")
        experts_in = sem("experts_in")
        x_res_in = [sem(f"x_res_in{j}") for j in range(2)]
        e_stats = sem("e_stats")
        e_var = sem("e_var")
        e_std = sem("e_std")
        e_rstd = sem("e_rstd")
        u_done = sem("u_done")
        u_gamma = sem("u_gamma")
        u_beta = sem("u_beta")
        x1_done = sem("x1_done")
        xf_done = sem("xf_done")
        acc_set = sem("acc_set")
        xfT_ready = sem("xfT_ready")
        xfT_done = sem("xfT_done")
        gate_ready = sem("gate_ready")
        best_done = sem("best_done")
        expert_ready = sem("expert_ready")
        mix_done = sem("mix_done")
        out_stored = [sem(f"out_stored{j}") for j in range(2)]

        block = ctx.enter_context(nc.Block())

        def carry_wait_dve():
            nc.vector.memset(tiny[:, 0:1], 0.0)
        known = lambda v: isinstance(v, int)

        def st_bank(n):
            return ps[:, n % 2, :]

        def mx_bank(n):
            return ps[:, 2 + 2 * (n % 2):4 + 2 * (n % 2), :]
        ZT_BANK, MISC = 6, 7

        def for_batches(eng, body):
            body(0)
            with eng.Fori(1, B - 1) as b:
                body(b)
            body(B - 1)

        @block.sync
        def _(sp):
            n = 0
            for dst, src in ((identity[:, :], identity_in), (wk[:, :, :], WkT.rearrange("(c p) o -> p c o", p=P)),
                             (wv[:, :, :], WvT.rearrange("(c p) o -> p c o", p=P)),
                             (wq[:, :, :], WqT.rearrange("(c p) o -> p c o", p=P)),
                             (bias_q[:, :], bq), (bias_k[:, :], bk),
                             (bias_v[:, :], bv.rearrange("(a d) -> a d", a=1).broadcast_to([P, D])),
                             (gate[:, :, :], gateT.rearrange("(c p) e -> p c e", p=P)),
                             (gamma_bc[:, :], gamma.rearrange("(a d) -> a d", a=1).broadcast_to([P, D])),
                             (beta_bc[:, :], beta.rearrange("(a d) -> a d", a=1).broadcast_to([P, D]))):
                if n == 1:
                    for j in range(2):
                        sp.dma_start(x_in[j], x_b[j]).then_inc(batch_in[j], LOADS)
                        sp.dma_start(ctx_in[j], ctxT_b[j]).then_inc(batch_in[j], LOADS)
                sp.dma_start(dst, src).then_inc(consts_in, LOADS)
                n += 1

            def phase1(p, last):
                for j in range(2):
                    n = 2 * p + j
                    sp.wait_ge(lo_done[0], n + 1)
                    sp.wait_ge(lo_done[1], n + 1)
                    sp.wait_ge(mid_done[0], n + 1)
                    sp.wait_ge(mid_done[1], n + 1)
                    for side, blocks in ((0, Q_BLOCKS), (1, K_BLOCKS)):
                        for i, part in enumerate(blocks):
                            sp.dma_start(op_scr[n, side, :, DH * i:DH * (i + 1), :].rearrange("m r (h s) -> (r h) m s", s=S),
                                         parts[j][:, side, part, :, :]).then_inc(op_stored[j], LOADS)
                    if not last:
                        sp.wait_ge(xn_done, n + 1)
                        sp.wait_ge(k_ready, n + 1)
                        sp.wait_ge(v_ready, n + 1)
                        sp.dma_start(x_in[j], x_b[n + 2]).then_inc(batch_in[j], LOADS)
                        sp.dma_start(ctx_in[j], ctxT_b[n + 2]).then_inc(batch_in[j], LOADS)

            with sp.Fori(0, B // 2 - 1) as p:
                phase1(p, False)
            phase1(B // 2 - 1, True)

            def load_op(b, g):
                for side, dst in ((0, q_op), (1, k_op)):
                    m, h0 = g * HG // HH, g * HG % HH
                    sp.dma_start(dst[0:ROWS, HG * g:HG * (g + 1), :],
                                 op_scr[b, side, m, :, h0 * S:(h0 + HG) * S].rearrange("r (h s) -> r h s", s=S)
                                 ).then_inc(op_loaded[g], LOADS)

            def load_shift(G, g, store):
                if store:
                    sp.wait_ge(sh_lo, G + 1)
                    sp.wait_ge(sh_hi, G + 1)
                    sp.dma_start(sh_scr[g % 2].rearrange("a r q -> r a q"), shift_parts[:, g % 2, :, :]).then_inc(sh_stored, LOADS)
                    sp.wait_ge(sh_stored, LOADS * (G + 1))
                    sp.dma_start(q_op[ROWS:SROWS, HG * g:HG * (g + 1), :],
                                 sh_scr[g % 2].rearrange("a (h t) q -> a h (t q)", t=TT)).then_inc(sh_loaded[g % 2], LOADS)

            for j in range(2):
                sp.wait_ge(op_stored[j], STORES * (B // 2))
            for g in range(3):
                load_op(0, g)
            load_shift(0, 0, True)

            def phase2(b):
                for g in range(NG):
                    G = NG * b + g
                    if not (known(G) and G + 3 >= GALL):
                        if not (known(G) and G == 0):
                            sp.wait_ge(st_ready, HG * TT * G)
                        load_op(b + (g + 3) // NG, (g + 3) % NG)
                    if not (known(G) and G + 1 >= GALL):
                        load_shift(G + 1, (g + 1) % NG, True)

            for_batches(sp, phase2)

            sp.wait_ge(v_aug_done, GALL)
            sp.dma_start(experts, expertT.rearrange("(c p) n -> p c n", p=P)).then_inc(experts_in, LOADS)
            sp.wait_ge(pv_done, GALL)
            for j in range(2):
                sp.dma_start(x_res[j], x_t[j]).then_inc(x_res_in[j], LOADS)

            def phase3(pair, last):
                for j in range(2):
                    T = 2 * pair + j
                    if not last:
                        sp.wait_ge(x1_done, T + 1)
                        sp.dma_start(x_res[j], x_t[T + 2]).then_inc(x_res_in[j], LOADS)
                    sp.wait_ge(mix_done, E * (T + 1))
                    sp.dma_start(out_t[T], acc[j]).then_inc(out_stored[j], LOADS)

            with sp.Fori(0, NT // 2 - 1) as pair:
                phase3(pair, False)
            phase3(NT // 2 - 1, True)
            for j in range(2):
                sp.wait_ge(out_stored[j], LOADS * (NT // 2))

        @block.gpsimd
        def _(pool):
            nc.gpsimd.memset(eps[:, :], EPS).then_inc(consts_set, 1)
            nc.gpsimd.memset(zeros[:, :], 0.0).then_inc(consts_set, 1)
            nc.gpsimd.memset(v_aug[:, :, :, :, :], 1.0).then_inc(consts_set, 1)
            pool.wait_ge(consts_set, 3)
            nc.gpsimd.memset(k_op[ROWS:P, :, :], 1.0).then_inc(consts_set, 1)
            pool.wait_ge(consts_set, 4)
            for e in range(E):
                nc.gpsimd.memset(rank_weight[:, e:e + 1], float(E - e)).then_inc(consts_set, 1)

            pool.wait_ge(consts_set, 4 + E)

            def phase1(p):
                for j in range(2):
                    n = 2 * p + j
                    pool.wait_ge(xn_done, n + 1)
                    nc.gpsimd.tensor_copy(normed[:, bass.ds(TT * n, TT), :], xn[j]).then_inc(xn_kept, 1)
                    for side in (1, 0):
                        pool.wait_ge(mid_done[side], n + 1)
                        pool.wait_ge(rest_done[side], KC * (n + 1))
                        if not (known(p) and p == 0):
                            pool.wait_ge(op_stored[j], STORES * p)
                        nc.gpsimd.tensor_tensor(parts[j][:, side, 2, :, :], rest[:, side, :, :], parts[j][:, side, 1, :, :],
                                                ALU.subtract).then_inc(lo_done[side], 1)

            phase1(0)
            with pool.Fori(1, B // 2) as p:
                phase1(p)

            def low_shift(G, i):
                pool.wait_ge(sh_rest, G + 1)
                if not (known(G) and G < 2):
                    pool.wait_ge(sh_stored, LOADS * (G - 1))
                nc.gpsimd.tensor_tensor(shift_parts[:, i, 1, :], shift_rest[:, i, :], zeros[:, :], ALU.add).then_inc(sh_mid, 1)
                pool.wait_ge(sh_mid, G + 1)
                nc.gpsimd.tensor_tensor(shift_parts[:, i, 2, :], shift_rest[:, i, :], shift_parts[:, i, 1, :],
                                        ALU.subtract).then_inc(sh_lo, 1)

            def add_z(G, tile, i):
                pool.wait_ge(recip_done, G + 1)
                nc.gpsimd.tensor_tensor(z_sb[:, i, :, :], zt[:, i, :, 0:DH],
                                        recip[:, i, :].rearrange("p (c a) -> p c a", a=1).broadcast_to([P, DH, DH]),
                                        ALU.mult).then_inc(z_done, 1)
                pool.wait_ge(z_done, G + 1)
                y = normed[:, tile, :].rearrange("p (c d) -> p c d", d=DH)
                nc.gpsimd.tensor_tensor(y, y, z_sb[:, i, :, :], ALU.add).then_inc(y_done, 1)

            pool.wait_ge(xn_kept, B)
            pool.wait_ge(v_done, B)
            low_shift(0, 0)

            def phase2(b):
                for g in range(NG):
                    G = NG * b + g
                    if not (known(G) and G < 2):
                        pool.wait_ge(pv_done, G - 1)
                    nc.gpsimd.tensor_copy(v_aug[:, g % 2, :, :, 0:DH],
                                          v_all[:, b, :, HG * DH * g:HG * DH * (g + 1)].rearrange("p t (h d) -> p t h d", d=DH)
                                          ).then_inc(v_aug_done, 1)
                    if not (known(G) and G + 1 >= GALL):
                        low_shift(G + 1, (g + 1) % 2)
                    if not (known(G) and G < 2):
                        add_z(G - 2, G - 2, g % 2)

            for_batches(pool, phase2)
            add_z(GALL - 2, GALL - 2, 0)
            add_z(GALL - 1, GALL - 1, 1)

            def start_sum(T, j, p):
                pool.wait_ge(xf_done, T + 1)
                if not (known(T) and T < 2):
                    pool.wait_ge(out_stored[j], LOADS * p)
                nc.gpsimd.tensor_tensor(acc[j], x1[j], xf[j], ALU.add).then_inc(acc_set, 1)

            def make_x1_at(p, j):
                T = 2 * p + j
                pool.wait_ge(u_done, T + 1)
                nc.gpsimd.tensor_tensor(u[j], u[j], gamma_bc[:, :], ALU.mult).then_inc(u_gamma, 1)
                pool.wait_ge(u_gamma, T + 1)
                nc.gpsimd.tensor_tensor(u[j], u[j], beta_bc[:, :], ALU.add).then_inc(u_beta, 1)
                pool.wait_ge(u_beta, T + 1)
                pool.wait_ge(x_res_in[j], LOADS * (p + 1))
                if not (known(T) and T < 2):
                    pool.wait_ge(xf_done, T - 1)
                nc.gpsimd.tensor_tensor(x1[j], u[j], x_res[j], ALU.add).then_inc(x1_done, 1)

            make_x1_at(0, 0)
            make_x1_at(0, 1)
            start_sum(0, 0, 0)

            def phase3(p):
                for j in range(2):
                    T = 2 * p + j
                    if not (known(T) and T + 1 >= NT):
                        start_sum(T + 1, 1 - j, p + j)
                    if not (known(T) and T + 2 >= NT):
                        make_x1_at(p + 1, j)

            phase3(0)
            with pool.Fori(1, NT // 2 - 1) as p:
                phase3(p)
            phase3(NT // 2 - 1)

        @block.scalar
        def _(act):
            act.wait_ge(consts_set, 4 + E)

            def take_std(n, j):
                act.wait_ge(var_done, n + 1)
                nc.scalar.activation(std[:, j, :], mv[:, j, :, 1], ACT.Sqrt, bias=eps[:, 0:1]).then_inc(std_done, 1)

            def high_and_mid(n, j, p, side, ready, bank, bias):
                act.wait_ge(ready, n + 1)
                if not (known(p) and p == 0):
                    act.wait_ge(op_stored[j], STORES * p)
                for m in range(KC):
                    nc.scalar.activation(parts[j][:, side, 0, m, :], ps[:, bank + m, :], ACT.Identity,
                                         bias=bias[:, m:m + 1]).then_inc(hi_done[side], 1)
                act.wait_ge(rest_done[side], KC * (n + 1))
                nc.scalar.activation(parts[j][:, side, 1, :, :], rest[:, side, :, :], ACT.Copy).then_inc(mid_done[side], 1)

            take_std(0, 0)
            act.wait_ge(consts_in, 10 * LOADS)

            def phase1(p, last):
                for j in range(2):
                    n = 2 * p + j
                    act.wait_ge(xT_ready, n + 1)
                    if not (known(p) and p == 0):
                        act.wait_ge(q_ready, n - 1)
                    nc.scalar.activation(xnT[j], ps[:, 0:KC, :], ACT.Copy).then_inc(xnT_done, 1)
                    high_and_mid(n, j, p, 1, k_ready, 4, bias_k)
                    if not (last and j == 1):
                        take_std(n + 1, 1 - j)
                    high_and_mid(n, j, p, 0, q_ready, 2, bias_q)

            phase1(0, False)
            with act.Fori(1, B // 2 - 1) as p:
                phase1(p, False)
            phase1(B // 2 - 1, True)

            for j in range(2):
                act.wait_ge(op_stored[j], STORES * (B // 2))
            act.wait_ge(xn_kept, B)

            def high_shift(G, i):
                act.wait_ge(maxT_ready, G + 1)
                if not (known(G) and G < 2):
                    act.wait_ge(sh_stored, LOADS * (G - 1))
                nc.scalar.activation(shift_parts[:, i, 0, :], ps[0:HG * TT, MISC, 0:P], ACT.Copy, scale=-1.0).then_inc(sh_hi, 1)

            high_shift(0, 0)

            def phase2(b):
                for g in range(NG):
                    G = NG * b + g
                    for h in range(HG):
                        for kt in range(TT):
                            n = HG * TT * G + TT * h + kt
                            act.wait_ge(st_ready, n + 1)
                            if h == 0 and kt == 0 and not (known(G) and G < 2):
                                act.wait_ge(pv_done, G - 1)
                            nc.scalar.activation(probs[:, g % 2, h, kt, :], st_bank(TT * h + kt), ACT.Exp).then_inc(exp_done, 1)
                            if h == 1 and kt == 1 and not (known(G) and G + 1 >= GALL):
                                high_shift(G + 1, (g + 1) % 2)

            for_batches(act, phase2)

            def e_take_std(k, j):
                act.wait_ge(e_var, k + 1)
                nc.scalar.activation(std[:, j, 0:1], mv[:, j, 0, 1:2], ACT.Sqrt, bias=eps[:, 0:1]).then_inc(e_std, 1)

            def take_xfT(T, j):
                act.wait_ge(xfT_ready, T + 1)
                if not (known(T) and T < 2):
                    act.wait_ge(expert_ready, (E // 2) * (T - 1))
                nc.scalar.activation(xfT[j], ps[:, 4, 0:D].rearrange("p (c s) -> p c s", c=KC), ACT.Copy).then_inc(xfT_done, 1)

            e_take_std(0, 0)
            e_take_std(1, 0)
            e_take_std(2, 1)
            take_xfT(0, 0)

            def phase3(p):
                for j in range(2):
                    T = 2 * p + j
                    if not (known(T) and T + 2 >= NT):
                        e_take_std(2 * T + 3, 0)
                    if not (known(T) and T + 1 >= NT):
                        e_take_std(2 * T + 4 if not (known(T) and T + 2 >= NT) else 2 * NT - 1, 1)
                        take_xfT(T + 1, 1 - j)

            phase3(0)
            with act.Fori(1, NT // 2 - 1) as p:
                phase3(p)
            phase3(NT // 2 - 1)

        @block.vector
        def _(dve):
            def norm_batch(n, j, p):
                dve.wait_ge(batch_in[j], 2 * LOADS * (p + 1))
                for t in range(TT):
                    nc.vector.bn_stats(bn[:, j, t, :], x_in[j][:, t, :]).then_inc(stats_step, 1)
                dve.wait_ge(stats_step, TT * (n + 1))
                carry_wait_dve()
                for t in range(TT):
                    ins = nc.vector.bn_aggr(mv[:, j, t, :], bn[:, j, t, :])
                ins.then_inc(var_done, 1)
                dve.wait_ge(std_done, n + 1)
                nc.vector.reciprocal(rstd[:, j, :], std[:, j, :]).then_inc(rstd_done, 1)
                dve.wait_ge(rstd_done, n + 1)
                dve.wait_ge(var_done, n + 1)
                if not (known(n) and n < 2):
                    dve.wait_ge(xT_ready, n - 1)
                    dve.wait_ge(xn_kept, n - 1)
                for t in range(TT):
                    ins = nc.vector.tensor_scalar(xn[j][:, t, :], x_in[j][:, t, :], mv[:, j, t, 0:1], rstd[:, j, t:t + 1],
                                                  ALU.subtract, ALU.mult)
                ins.then_inc(xn_done, 1)

            def take_rest(n, j, side, bank, bias):
                if not (known(n) and n == 0):
                    dve.wait_ge(lo_done[side], n)
                    dve.wait_ge(mid_done[side], n)
                for m in range(KC):
                    dve.wait_ge(hi_done[side], KC * n + m + 1)
                    nc.vector.scalar_tensor_tensor(rest[:, side, m, :], ps[:, bank + m, :], bias[:, m:m + 1],
                                                   parts[j][:, side, 0, m, :], ALU.add, ALU.subtract).then_inc(rest_done[side], 1)

            norm_batch(0, 0, 0)
            dve.wait_ge(consts_in, 10 * LOADS)

            def phase1(p, last):
                for j in range(2):
                    n = 2 * p + j
                    take_rest(n, j, 1, 4, bias_k)
                    dve.wait_ge(v_ready, n + 1)
                    for i in range(2):
                        ins = nc.vector.tensor_tensor(v_all[:, n, 2 * i:2 * i + 2, :],
                                                      ps[:, 6 + i, :].rearrange("p (t d) -> p t d", t=2),
                                                      bias_v[:, :].rearrange("p (a d) -> p a d", a=1).broadcast_to([P, 2, D]), ALU.add)
                    ins.then_inc(v_done, 1)
                    if not (last and j == 1):
                        norm_batch(n + 1, 1 - j, p + j)
                    take_rest(n, j, 0, 2, bias_q)

            phase1(0, False)
            with dve.Fori(1, B // 2 - 1) as p:
                phase1(p, False)
            phase1(B // 2 - 1, True)

            def row_maxima(G, i, unit):
                dve.wait_ge(scores_ready, 2 * HG * G + unit + 1)
                if unit == 0 and not (known(G) and G < 2):
                    dve.wait_ge(maxT_ready, G - 1)
                nc.vector.reduce_max(row_max[:, i, 2 * unit:2 * unit + 2], mx_bank(unit), AX_X).then_inc(max_done, 1)

            def rest_shift(G, i):
                dve.wait_ge(sh_hi, G + 1)
                if not (known(G) and G < 2):
                    dve.wait_ge(sh_lo, G - 1)
                nc.vector.scalar_tensor_tensor(shift_rest[:, i, :], ps[0:HG * TT, MISC, 0:P], -1.0, shift_parts[:, i, 0, :],
                                               ALU.mult, ALU.subtract).then_inc(sh_rest, 1)

            def token_major(G, i):
                dve.wait_ge(pv_done, G + 1)
                if not (known(G) and G < 2):
                    dve.wait_ge(z_done, G - 1)
                nc.vector.transpose(zt[:, i, :, :], ps[:, ZT_BANK, :].rearrange("p (a c) -> p c a", c=DH)).then_inc(zt_done, 1)
                dve.wait_ge(zt_done, G + 1)
                nc.vector.reciprocal(recip[:, i, :], zt[:, i, :, DH]).then_inc(recip_done, 1)

            for unit in range(2 * HG):
                row_maxima(0, 0, unit)
            rest_shift(0, 0)
            for unit in range(2 * HG):
                row_maxima(1, 1, unit)

            def phase2(b):
                for g in range(NG):
                    G = NG * b + g
                    if not (known(G) and G < 2):
                        token_major(G - 2, g % 2)
                    for unit in range(2 * HG):
                        if not (known(G) and G + 2 >= GALL):
                            row_maxima(G + 2, g % 2, unit)
                        if unit == 1 and not (known(G) and G + 1 >= GALL):
                            rest_shift(G + 1, (g + 1) % 2)

            for_batches(dve, phase2)
            token_major(GALL - 2, 0)
            token_major(GALL - 1, 1)

            def e_norm(k, j, src, dst):
                nc.vector.bn_stats(bn[:, j, 0, :], src).then_inc(e_stats, 1)
                dve.wait_ge(e_stats, k + 1)
                carry_wait_dve()
                nc.vector.bn_aggr(mv[:, j, 0, :], bn[:, j, 0, :]).then_inc(e_var, 1)
                dve.wait_ge(e_std, k + 1)
                nc.vector.reciprocal(rstd[:, j, 0:1], std[:, j, 0:1]).then_inc(e_rstd, 1)
                dve.wait_ge(e_rstd, k + 1)
                dve.wait_ge(e_var, k + 1)
                return nc.vector.tensor_scalar(dst, src, mv[:, j, 0, 0:1], rstd[:, j, 0:1], ALU.subtract, ALU.mult)

            def stage_a(T, j, k):
                if not (known(T) and T < 2):
                    dve.wait_ge(x1_done, T - 1)
                e_norm(k, 0, normed[:, T, :], u[j]).then_inc(u_done, 1)

            def stage_b(T, j, k):
                dve.wait_ge(x1_done, T + 1)
                if not (known(T) and T < 2):
                    dve.wait_ge(acc_set, T - 1)
                    dve.wait_ge(xfT_ready, T - 1)
                e_norm(k, 1, x1[j], xf[j]).then_inc(xf_done, 1)

            best = smalls[:, 0:1]
            tied = smalls[:, 8:8 + E]
            first = smalls[:, 16:17]
            chosen = smalls[:, 24:24 + E]

            def choose(T):
                dve.wait_ge(gate_ready, T + 1)
                nc.vector.reduce_max(best, ps[:, 5, 0:E], AX_X).then_inc(best_done, 1)
                dve.wait_ge(best_done, 4 * T + 1)
                nc.vector.scalar_tensor_tensor(tied, ps[:, 5, 0:E], best, rank_weight[:, :], ALU.is_equal, ALU.mult).then_inc(best_done, 1)
                dve.wait_ge(best_done, 4 * T + 2)
                nc.vector.reduce_max(first, tied, AX_X).then_inc(best_done, 1)
                dve.wait_ge(best_done, 4 * T + 3)
                nc.vector.tensor_scalar(chosen, rank_weight[:, :], first, None, ALU.is_equal).then_inc(best_done, 1)
                dve.wait_ge(best_done, 4 * T + 4)

            def mix(T, j):
                dve.wait_ge(acc_set, T + 1)
                for e in range(E):
                    if e % 2 == 0:
                        dve.wait_ge(expert_ready, (E // 2) * T + e // 2 + 1)
                    if e:
                        dve.wait_ge(mix_done, E * T + e)
                    nc.vector.scalar_tensor_tensor(acc[j], ps[:, e // 2, (e % 2) * D:(e % 2 + 1) * D], chosen[:, e:e + 1],
                                                   acc[j], ALU.mult, ALU.add).then_inc(mix_done, 1)

            dve.wait_ge(y_done, GALL)
            dve.wait_ge(pv_done, GALL)
            stage_a(0, 0, 0)
            stage_a(1, 1, 1)
            stage_b(0, 0, 2)

            def phase3(p):
                for j in range(2):
                    T = 2 * p + j
                    ahead = not (known(T) and T + 2 >= NT)
                    if ahead:
                        stage_a(T + 2, j, 2 * T + 3)
                    if not (known(T) and T + 1 >= NT):
                        stage_b(T + 1, 1 - j, 2 * T + 4 if ahead else 2 * NT - 1)
                    choose(T)
                    mix(T, j)

            phase3(0)
            with dve.Fori(1, NT // 2 - 1) as p:
                phase3(p)
            phase3(NT // 2 - 1)

        @block.tensor
        def _(pe):
            pe.wait_ge(consts_in, 10 * LOADS)

            def phase1(p):
                for j in range(2):
                    n = 2 * p + j
                    first = known(n) and n == 0
                    pe.wait_ge(xn_done, n + 1)
                    if not first:
                        pe.wait_ge(xnT_done, n)
                    for t in range(TT):
                        for c in range(KC):
                            ins = nc.tensor.transpose(ps[:, c, t * P:(t + 1) * P], xn[j][:, t, c * P:(c + 1) * P], identity[:, :])
                    ins.then_inc(xT_ready, 1)
                    pe.wait_ge(batch_in[j], 2 * LOADS * (p + 1))
                    if not first:
                        pe.wait_ge(rest_done[1], KC * n)
                    for m in range(KC):
                        for c in range(KC):
                            ins = nc.tensor.matmul(ps[:, 4 + m, :], wk[:, c, m * P:(m + 1) * P], ctx_in[j][:, c, :],
                                                   start=(c == 0), stop=(c == KC - 1))
                    ins.then_inc(k_ready, 1)
                    if not first:
                        pe.wait_ge(v_done, n)
                    for t in range(TT):
                        for c in range(KC):
                            ins = nc.tensor.matmul(ps[:, 6 + t // 2, (t % 2) * D:(t % 2 + 1) * D],
                                                   ctx_in[j][:, c, t * P:(t + 1) * P], wv[:, c, :],
                                                   start=(c == 0), stop=(c == KC - 1))
                    ins.then_inc(v_ready, 1)
                    pe.wait_ge(xnT_done, n + 1)
                    if not first:
                        pe.wait_ge(rest_done[0], KC * n)
                    for m in range(KC):
                        for c in range(KC):
                            ins = nc.tensor.matmul(ps[:, 2 + m, :], wq[:, c, m * P:(m + 1) * P], xnT[j][:, c, :],
                                                   start=(c == 0), stop=(c == KC - 1))
                    ins.then_inc(q_ready, 1)

            phase1(0)
            with pe.Fori(1, B // 2) as p:
                phase1(p)
            pe.wait_ge(rest_done[0], KC * B)
            pe.wait_ge(rest_done[1], KC * B)
            pe.wait_ge(v_done, B)
            pe.wait_ge(xnT_done, B)
            pe.wait_ge(consts_set, 4 + E)

            def score(G, g, h, qt):
                unit = 2 * h + qt // 2
                if qt % 2 == 0:
                    if h == 0 and qt == 0:
                        b = G_batch(G)
                        pe.wait_ge(op_loaded[g], 2 * LOADS * (b + 1))
                    if not (known(G) and G == 0 and unit < 2):
                        pe.wait_ge(max_done, 2 * HG * G + unit - 1)
                hd = HG * g + h
                ins = nc.tensor.matmul(mx_bank(unit)[:, qt % 2, :], q_op[0:ROWS, hd, qt * P:(qt + 1) * P], k_op[0:ROWS, hd, :],
                                       start=True, stop=True)
                if qt % 2:
                    ins.then_inc(scores_ready, 1)

            def shifted(G, g, h, kt):
                n = TT * h + kt
                if n == 0:
                    pe.wait_ge(sh_loaded[g % 2], LOADS * G_pair(G))
                if not (known(G) and G == 0 and n < 2):
                    pe.wait_ge(exp_done, HG * TT * G + n - 1)
                hd = HG * g + h
                nc.tensor.matmul(st_bank(n), k_op[0:SROWS, hd, kt * P:(kt + 1) * P], q_op[0:SROWS, hd, :],
                                 start=True, stop=True).then_inc(st_ready, 1)

            def transpose_max(G, i):
                pe.wait_ge(max_done, 2 * HG * (G + 1))
                if not (known(G) and G < 1):
                    pe.wait_ge(sh_rest, G)
                nc.tensor.transpose(ps[0:HG * TT, MISC, 0:P], row_max[:, i, :], identity[:, :]).then_inc(maxT_ready, 1)

            def attend(G, i, kt):
                if kt == 0:
                    pe.wait_ge(v_aug_done, G + 1)
                    if not (known(G) and G == 0):
                        pe.wait_ge(zt_done, G)
                pe.wait_ge(exp_done, HG * TT * G + (HG - 1) * TT + kt + 1)
                for h in range(HG):
                    ins = nc.tensor.matmul(ps[2 * DH * h:2 * DH * (h + 1), ZT_BANK, :], v_aug[:, i, kt, h, :],
                                           probs[:, i, h, kt, :], start=(kt == 0), stop=(kt == TT - 1),
                                           tile_position=(0, 2 * DH * h))
                if kt == TT - 1:
                    ins.then_inc(pv_done, 1)

            batch_of = {}

            def G_batch(G):
                return G // NG if known(G) else batch_of["b"]

            def G_pair(G):
                return G // 2 + 1 if known(G) else 2 * batch_of["b"] + batch_of["g"] // 2 + 1

            def score_unit(G, g, h, half):
                for qt in (2 * half, 2 * half + 1):
                    score(G, g, h, qt)

            for h in range(HG):
                for half in range(2):
                    score_unit(0, 0, h, half)
            transpose_max(0, 0)
            for h in range(HG):
                for half in range(2):
                    score_unit(1, 1, h, half)

            def phase2(b):
                for g in range(NG):
                    G = NG * b + g

                    def mx(h, half):
                        if not (known(G) and G + 2 >= GALL):
                            batch_of["b"] = b + (g + 2) // NG
                            score_unit(G + 2, (g + 2) % NG, h, half)

                    def st(h, kt):
                        batch_of["b"], batch_of["g"] = b, g
                        shifted(G, g, h, kt)

                    for h in range(HG):
                        st(h, 0)
                        st(h, 1)
                        mx(h, 0)
                        if not (known(G) and G == 0):
                            attend(G - 1, (g + 1) % 2, h)
                        st(h, 2)
                        if h == 0 and not (known(G) and G + 1 >= GALL):
                            transpose_max(G + 1, (g + 1) % 2)
                        mx(h, 1)
                        st(h, 3)

            for_batches(pe, phase2)
            for kt in range(TT):
                attend(GALL - 1, 1, kt)

            def transpose_xf(T, j):
                pe.wait_ge(xf_done, T + 1)
                if not (known(T) and T == 0):
                    pe.wait_ge(xfT_done, T)
                for c in range(KC):
                    ins = nc.tensor.transpose(ps[:, 4, c * P:(c + 1) * P], xf[j][:, c * P:(c + 1) * P], identity[:, :])
                ins.then_inc(xfT_ready, 1)

            def gates(T, j):
                pe.wait_ge(xfT_done, T + 1)
                if not (known(T) and T == 0):
                    pe.wait_ge(best_done, 4 * T)
                for c in range(KC):
                    ins = nc.tensor.matmul(ps[:, 5, 0:E], xfT[j][:, c, :], gate[:, c, :], start=(c == 0), stop=(c == KC - 1))
                ins.then_inc(gate_ready, 1)

            def expert_pair(T, j, i):
                if not (known(T) and T == 0):
                    pe.wait_ge(mix_done, E * (T - 1) + 2 * i + 2)
                for c in range(KC):
                    ins = nc.tensor.matmul(ps[:, i, :], xfT[j][:, c, :], experts[:, c, 2 * D * i:2 * D * (i + 1)],
                                           start=(c == 0), stop=(c == KC - 1))
                ins.then_inc(expert_ready, 1)

            pe.wait_ge(experts_in, LOADS)
            pe.wait_ge(exp_done, HG * TT * GALL)
            pe.wait_ge(max_done, 2 * HG * GALL)
            transpose_xf(0, 0)
            gates(0, 0)

            def phase3(p):
                for j in range(2):
                    T = 2 * p + j
                    more = not (known(T) and T + 1 >= NT)
                    for i in range(E // 2):
                        expert_pair(T, j, i)
                        if i == 1 and more:
                            transpose_xf(T + 1, 1 - j)
                    if more:
                        gates(T + 1, 1 - j)

            phase3(0)
            with pe.Fori(1, NT // 2 - 1) as p:
                phase3(p)
            phase3(NT // 2 - 1)


def kernel(x, ctx_1024, L0_xattn_Wq, L0_xattn_bq, L0_xattn_Wk, L0_xattn_bk, L0_xattn_Wv, L0_xattn_bv,
           L0_xattn_gamma, L0_xattn_beta, L0_ffn_gate_w, L0_ffn_expert_w):
    import numpy as np
    import concourse.bacc as bacc
    from concourse.bass_utils import run_bass_kernel_spmd

    D = x.shape[-1]
    dh = D // H
    half = P // dh
    order = np.array([(m * half + p % half) * dh + p // half for m in range(D // P) for p in range(P)])
    c = np.ascontiguousarray
    arrays = {
        "x": c(x),
        "ctxT": c(np.transpose(np.asarray(ctx_1024), (0, 2, 1))),
        "WqT": c(np.asarray(L0_xattn_Wq)[order].T),
        "bq": c(np.asarray(L0_xattn_bq)[order].reshape(D // P, P).T),
        "WkT": c(np.asarray(L0_xattn_Wk)[order].T),
        "bk": c(np.asarray(L0_xattn_bk)[order].reshape(D // P, P).T),
        "WvT": c(np.asarray(L0_xattn_Wv).T),
        "bv": c(L0_xattn_bv),
        "gamma": c(L0_xattn_gamma),
        "beta": c(L0_xattn_beta),
        "gateT": c(np.asarray(L0_ffn_gate_w).T),
        "expertT": c(np.transpose(np.asarray(L0_ffn_expert_w), (2, 0, 1)).reshape(D, -1)),
        "identity_in": np.eye(P, dtype=np.float32),
    }
    nc = bacc.Bacc("TRN2", target_bir_lowering=False, num_devices=1)
    args = [nc.dram_tensor(f"in_{k}", a.shape, mybir.dt.from_np(a.dtype), kind="ExternalInput").ap() for k, a in arrays.items()]
    out = nc.dram_tensor("out_0", x.shape, F32, kind="ExternalOutput").ap()
    xattn_ffn_kernel(nc, *args, out)
    r = run_bass_kernel_spmd(nc, [{f"in_{k}": a for k, a in arrays.items()}], core_ids=[0])
    return r.results[0]["out_0"]
```

```python
from contextlib import ExitStack

import concourse.bass as bass
from concourse import mybir

P = 128
F32 = mybir.dt.float32
F32R = mybir.dt.float32r
BF16 = mybir.dt.bfloat16
ALU = mybir.AluOpType
ACT = mybir.ActivationFunctionType
AX_X = mybir.AxisListType.X

H = 16
EPS = 1e-5
Q_BLOCKS = (0, 0, 1, 1, 0, 2)
K_BLOCKS = (0, 1, 0, 1, 2, 0)
NBLK = len(Q_BLOCKS)


def xattn_ffn_kernel(nc: bass.Bass, x, ctxT, WqT, bq, WkT, bk, WvT, bv, gamma, beta, gateT, expertT, identity_in, out):
    B, S, D = x.shape
    DH = D // H
    TT = S // P
    KC = D // P
    E = gateT.shape[1]
    HG = 4
    NG = H // HG
    GALL = B * NG
    HH = H // KC
    ROWS = NBLK * DH
    SROWS = ROWS + 3
    NT = B * TT
    LOADS = 16

    with ExitStack() as ctx:
        def sb(name, shape, dt=F32):
            return ctx.enter_context(nc.sbuf_tensor(name, shape, dt))

        def sem(name):
            return ctx.enter_context(nc.semaphore(name))

        identity = sb("identity", [P, P])
        wq = sb("wq", [P, KC, D])
        wk = sb("wk", [P, KC, D])
        wv = sb("wv", [P, KC, D])
        bias_q = sb("bias_q", [P, KC])
        bias_k = sb("bias_k", [P, KC])
        bias_v = sb("bias_v", [P, D])
        gamma_bc = sb("gamma_bc", [P, D])
        beta_bc = sb("beta_bc", [P, D])
        tiny = sb("tiny", [P, 1])
        zeros = sb("zeros", [P, 32])
        eps = sb("eps", [P, 1])
        rank_weight = sb("rank_weight", [P, E])
        normed = sb("normed", [P, NT, D])
        NE = E * D + E
        v_offset = nc.sbuf_base + (-nc.sbuf_base) % 32
        v_flat = sb("v_all", [P, 2 * KC * NE])
        v_all = v_flat[:, 0:B * TT * D].rearrange("p (b t d) -> p b t d", b=B, t=TT)
        experts = v_flat[:, 0:KC * NE].rearrange("p (c n) -> p c n", c=KC)
        experts_hi = sb("experts_hi", [P, KC, NE], F32R)
        experts_lo = nc.alloc_sbuf_tensor_at("experts_lo", [P, KC, NE], F32R,
                                             offset=v_offset + 4 * KC * NE)
        xfT_hi = sb("xfT_hi", [P, 2, KC, P], F32R)
        xfT_lo = sb("xfT_lo", [P, 2, KC, P], F32R)
        work = sb("work", [P, 16384])
        q_op = sb("q_op", [P, H, S], BF16)
        k_op = sb("k_op", [P, H, S], BF16)
        v_aug = sb("v_aug", [P, 2, TT, HG, 2 * DH])
        zT = sb("zT", [P, 2, S])
        zt = sb("zt", [P, 2, DH, 2 * DH])
        z_sb = sb("z_sb", [P, 2, DH, DH])
        row_max = sb("row_max", [P, 2, 32])
        maxT = sb("maxT", [P, 2, 32])
        shift = sb("shift", [P, 2, 32])
        recip = sb("recip", [P, 2, DH])
        shift_parts = sb("shift_parts", [P, 2, 3, 32], BF16)
        shift_rest = sb("shift_rest", [P, 2, 32])
        bn = sb("bn", [P, 2, TT, 6])
        mv = sb("mv", [P, 2, TT, 2])
        std = sb("std", [P, 2, TT])
        rstd = sb("rstd", [P, 2, TT])
        ps = ctx.enter_context(nc.psum_tensor("ps", [P, 8, 512], F32))

        off = [0]

        def take(n):
            off[0] += n
            return work[:, off[0] - n:off[0]]

        x_in = [take(TT * D).rearrange("p (t d) -> p t d", t=TT) for _ in range(2)]
        xn = [take(TT * D).rearrange("p (t d) -> p t d", t=TT) for _ in range(2)]
        xnT = [take(KC * S).rearrange("p (c s) -> p c s", c=KC) for _ in range(2)]
        ctx_in = [take(KC * S).rearrange("p (c s) -> p c s", c=KC) for _ in range(2)]
        parts = [take(2 * 3 * KC * S // 2).bitcast(BF16).rearrange("p (q a m s) -> p q a m s", q=2, a=3, m=KC)
                 for _ in range(2)]
        rest = take(2 * KC * S).rearrange("p (q m s) -> p q m s", q=2, m=KC)
        probs = work[:, :].rearrange("p (g h k q) -> p g h k q", g=2, h=HG, k=TT)
        x_res = [work[:, i * D:(i + 1) * D] for i in (0, 1)]
        u = [work[:, i * D:(i + 1) * D] for i in (2, 3)]
        x1 = [work[:, i * D:(i + 1) * D] for i in (4, 5)]
        xf = [work[:, i * D:(i + 1) * D] for i in (6, 7)]
        even = [work[:, i * D:(i + 1) * D] for i in (8, 9)]
        odd = [work[:, i * D:(i + 1) * D] for i in (10, 11)]
        scaled = [work[:, i * D:(i + 2) * D].rearrange("p (e d) -> p e d", e=2) for i in (14, 16)]
        result = [work[:, i * D:(i + 1) * D] for i in (18, 19)]
        smalls = work[:, 12 * D:13 * D]
        best = smalls[:, 0:1]
        tied = smalls[:, 8:8 + E]
        first = smalls[:, 16:17]
        chosen = [smalls[:, i:i + E] for i in (24, 32)]

        op_scr = nc.dram_tensor("op_scr", [B, 2, KC, ROWS, HH * S], BF16, kind="Internal").ap()
        sh_scr = nc.dram_tensor("sh_scr", [2, 3, P, 32], BF16, kind="Internal").ap()

        x_b = x.rearrange("b (t p) d -> b p t d", p=P)
        ctxT_b = ctxT.rearrange("b (c p) s -> b p c s", p=P)
        x_t = x.rearrange("b (t p) d -> (b t) p d", p=P)
        out_t = out.rearrange("b (t p) d -> (b t) p d", p=P)

        consts_in = sem("consts_in")
        consts_set = sem("consts_set")
        batch_in = [sem(f"batch_in{j}") for j in range(2)]
        var_done = sem("var_done")
        stats_step = sem("stats_step")
        std_done = sem("std_done")
        rstd_done = sem("rstd_done")
        xn_done = sem("xn_done")
        xn_kept = sem("xn_kept")
        xT_ready = sem("xT_ready")
        xnT_done = sem("xnT_done")
        k_ready = sem("k_ready")
        v_ready = sem("v_ready")
        q_ready = sem("q_ready")
        hi_done = [sem("hi_q"), sem("hi_k")]
        rest_done = [sem("rest_q"), sem("rest_k")]
        mid_done = [sem("mid_q"), sem("mid_k")]
        lo_done = [sem("lo_q"), sem("lo_k")]
        v_done = sem("v_done")
        op_stored = [sem(f"op_stored{j}") for j in range(2)]
        STORES = 2 * NBLK * LOADS
        op_loaded = [sem(f"op_loaded{g}") for g in range(NG)]
        scores_ready = sem("scores_ready")
        max_done = sem("max_done")
        maxT_ready = sem("maxT_ready")
        shift_set = sem("shift_set")
        sh_hi = sem("sh_hi")
        sh_rest = sem("sh_rest")
        sh_mid = sem("sh_mid")
        sh_lo = sem("sh_lo")
        sh_stored = sem("sh_stored")
        sh_loaded = [sem(f"sh_loaded{j}") for j in range(2)]
        st_ready = sem("st_ready")
        exp_done = sem("exp_done")
        v_aug_done = sem("v_aug_done")
        pv_done = sem("pv_done")
        zT_done = sem("zT_done")
        zt_done = sem("zt_done")
        recip_done = sem("recip_done")
        z_done = sem("z_done")
        y_done = sem("y_done")
        experts_in = sem("experts_in")
        x_res_in = [sem(f"x_res_in{j}") for j in range(2)]
        experts_cut = sem("experts_cut")
        experts_ready = sem("experts_ready")
        e_stats = sem("e_stats")
        e_var = sem("e_var")
        e_std = sem("e_std")
        e_rstd = sem("e_rstd")
        u_done = sem("u_done")
        u_gamma = sem("u_gamma")
        u_beta = sem("u_beta")
        x1_done = sem("x1_done")
        xf_done = sem("xf_done")
        even_set = sem("even_set")
        xfT_ready = sem("xfT_ready")
        xfT_high = sem("xfT_high")
        xfT_low = sem("xfT_low")
        gate_ready = sem("gate_ready")
        best_done = sem("best_done")
        expert_ready = sem("expert_ready")
        mix_done = sem("mix_done")
        scaled_done = sem("scaled_done")
        sum_done = sem("sum_done")
        out_stored = [sem(f"out_stored{j}") for j in range(2)]
        MIX = E - 2

        block = ctx.enter_context(nc.Block())

        def carry_wait_dve():
            nc.vector.memset(tiny[:, 0:1], 0.0)
        known = lambda v: isinstance(v, int)

        ST_BANKS = (0, 1, 7)
        ST_BATCH = NG * HG * TT

        def st_bank(n):
            return ps[:, ST_BANKS[n % 3], :]

        def st_before(n):
            return n - 2 if n >= 3 else max(m for m in range(-ST_BATCH, 0) if (m + ST_BATCH) % 3 == n % 3) + 1

        def mx_bank(n):
            return ps[:, 2 + 2 * (n % 2):4 + 2 * (n % 2), :]
        ZT_BANK = 6

        def for_batches(eng, body):
            body(0)
            with eng.Fori(1, B - 1) as b:
                body(b)
            body(B - 1)

        @block.sync
        def _(sp):
            n = 0
            for dst, src in ((identity[:, :], identity_in), (wk[:, :, :], WkT.rearrange("(c p) o -> p c o", p=P)),
                             (wv[:, :, :], WvT.rearrange("(c p) o -> p c o", p=P)),
                             (wq[:, :, :], WqT.rearrange("(c p) o -> p c o", p=P)),
                             (bias_q[:, :], bq), (bias_k[:, :], bk),
                             (bias_v[:, :], bv.rearrange("(a d) -> a d", a=1).broadcast_to([P, D])),
                             (gamma_bc[:, :], gamma.rearrange("(a d) -> a d", a=1).broadcast_to([P, D])),
                             (beta_bc[:, :], beta.rearrange("(a d) -> a d", a=1).broadcast_to([P, D]))):
                if n == 1:
                    for j in range(2):
                        sp.dma_start(x_in[j], x_b[j]).then_inc(batch_in[j], LOADS)
                        sp.dma_start(ctx_in[j], ctxT_b[j]).then_inc(batch_in[j], LOADS)
                sp.dma_start(dst, src).then_inc(consts_in, LOADS)
                n += 1

            def phase1(p, last):
                for j in range(2):
                    n = 2 * p + j
                    if not last:
                        sp.wait_ge(xn_done, n + 1)
                        sp.wait_ge(k_ready, n + 1)
                        sp.wait_ge(v_ready, n + 1)
                        sp.dma_start(x_in[j], x_b[n + 2]).then_inc(batch_in[j], LOADS)
                        sp.dma_start(ctx_in[j], ctxT_b[n + 2]).then_inc(batch_in[j], LOADS)
                    sp.wait_ge(lo_done[0], n + 1)
                    sp.wait_ge(lo_done[1], n + 1)
                    sp.wait_ge(mid_done[0], n + 1)
                    sp.wait_ge(mid_done[1], n + 1)
                    for side, blocks in ((0, Q_BLOCKS), (1, K_BLOCKS)):
                        for i, part in enumerate(blocks):
                            sp.dma_start(op_scr[n, side, :, DH * i:DH * (i + 1), :].rearrange("m r (h s) -> (r h) m s", s=S),
                                         parts[j][:, side, part, :, :]).then_inc(op_stored[j], LOADS)

            with sp.Fori(0, B // 2 - 1) as p:
                phase1(p, False)
            phase1(B // 2 - 1, True)

            def load_op(b, g):
                for side, dst in ((0, q_op), (1, k_op)):
                    m, h0 = g * HG // HH, g * HG % HH
                    sp.dma_start(dst[0:ROWS, HG * g:HG * (g + 1), :],
                                 op_scr[b, side, m, :, h0 * S:(h0 + HG) * S].rearrange("r (h s) -> r h s", s=S)
                                 ).then_inc(op_loaded[g], LOADS)

            def load_shift(G, g, store):
                if store:
                    sp.wait_ge(sh_lo, G + 1)
                    sp.wait_ge(sh_hi, G + 1)
                    sp.dma_start(sh_scr[g % 2].rearrange("a p q -> p a q"), shift_parts[:, g % 2, :, :]).then_inc(sh_stored, LOADS)
                    sp.wait_ge(sh_stored, LOADS * (G + 1))
                    for part in range(3):
                        sp.dma_start(q_op[ROWS + part:ROWS + part + 1, HG * g:HG * (g + 1), :].rearrange(
                                         "x h (t a r) -> x (h t) a r", a=4, r=32),
                                     sh_scr[g % 2, part:part + 1].rearrange("x (a c) r -> x c a r", a=4)[:, 0:HG * TT, :, :]
                                     ).then_inc(sh_loaded[g % 2], LOADS)

            for j in range(2):
                sp.wait_ge(op_stored[j], STORES * (B // 2))
            for g in range(3):
                load_op(0, g)
            load_shift(0, 0, True)

            def phase2(b):
                if known(b) and b == B - 1:
                    sp.wait_ge(v_aug_done, NG * (B - 1))
                    sp.dma_start(experts[:, :, 0:E * D], expertT.rearrange("(c p) n -> p c n", p=P)).then_inc(experts_in, LOADS)
                    sp.dma_start(experts[:, :, E * D:NE], gateT.rearrange("(c p) e -> p c e", p=P)).then_inc(experts_in, LOADS)
                for g in range(NG):
                    G = NG * b + g
                    if not (known(G) and G + 3 >= GALL):
                        if not (known(G) and G == 0):
                            sp.wait_ge(st_ready, HG * TT * G)
                        load_op(b + (g + 3) // NG, (g + 3) % NG)
                    if not (known(G) and G + 1 >= GALL):
                        load_shift(G + 1, (g + 1) % NG, True)

            for_batches(sp, phase2)

            sp.wait_ge(pv_done, GALL)
            for j in range(2):
                sp.dma_start(x_res[j], x_t[j]).then_inc(x_res_in[j], LOADS)

            for j in range(2):
                sp.wait_ge(x1_done, j + 1)
                sp.dma_start(x_res[j], x_t[2 + j]).then_inc(x_res_in[j], LOADS)

            def phase3(pair, last):
                for j in range(2):
                    T = 2 * pair + j
                    if not last:
                        sp.wait_ge(x1_done, T + 3)
                        sp.dma_start(x_res[j], x_t[T + 4]).then_inc(x_res_in[j], LOADS)
                    sp.wait_ge(sum_done, 3 * (T + 1))
                    sp.dma_start(out_t[T], result[j]).then_inc(out_stored[j], LOADS)

            with sp.Fori(0, NT // 2 - 2) as pair:
                phase3(pair, False)
            phase3(NT // 2 - 2, True)
            phase3(NT // 2 - 1, True)
            for j in range(2):
                sp.wait_ge(out_stored[j], LOADS * (NT // 2))

        @block.gpsimd
        def _(pool):
            nc.gpsimd.memset(eps[:, :], EPS).then_inc(consts_set, 1)
            nc.gpsimd.memset(zeros[:, :], 0.0).then_inc(consts_set, 1)
            nc.gpsimd.memset(row_max[:, :, :], 0.0).then_inc(consts_set, 1)
            nc.gpsimd.memset(v_aug[:, :, :, :, :], 1.0).then_inc(consts_set, 1)
            pool.wait_ge(consts_set, 4)
            nc.gpsimd.memset(k_op[ROWS:P, :, :], 1.0).then_inc(consts_set, 1)
            pool.wait_ge(consts_set, 5)
            for e in range(E):
                nc.gpsimd.memset(rank_weight[:, e:e + 1], float(E - e)).then_inc(consts_set, 1)

            pool.wait_ge(consts_set, 5 + E)

            def phase1(p):
                for j in range(2):
                    n = 2 * p + j
                    pool.wait_ge(xn_done, n + 1)
                    nc.gpsimd.tensor_copy(normed[:, bass.ds(TT * n, TT), :], xn[j]).then_inc(xn_kept, 1)
                    for side in (1, 0):
                        pool.wait_ge(mid_done[side], n + 1)
                        pool.wait_ge(rest_done[side], KC * (n + 1))
                        if not (known(p) and p == 0):
                            pool.wait_ge(op_stored[j], STORES * p)
                        nc.gpsimd.tensor_tensor(parts[j][:, side, 2, :, :], rest[:, side, :, :], parts[j][:, side, 1, :, :],
                                                ALU.subtract).then_inc(lo_done[side], 1)

            phase1(0)
            with pool.Fori(1, B // 2) as p:
                phase1(p)

            def low_shift(G, i):
                pool.wait_ge(sh_hi, G + 1)
                pool.wait_ge(shift_set, G + 1)
                nc.gpsimd.tensor_tensor(shift_rest[:, i, :], shift[:, i, :], shift_parts[:, i, 0, :],
                                        ALU.subtract).then_inc(sh_rest, 1)
                pool.wait_ge(sh_rest, G + 1)
                nc.gpsimd.tensor_tensor(shift_parts[:, i, 1, :], shift_rest[:, i, :], zeros[:, :], ALU.add).then_inc(sh_mid, 1)
                pool.wait_ge(sh_mid, G + 1)
                nc.gpsimd.tensor_tensor(shift_parts[:, i, 2, :], shift_rest[:, i, :], shift_parts[:, i, 1, :],
                                        ALU.subtract).then_inc(sh_lo, 1)

            def add_z(G, tile, i):
                pool.wait_ge(recip_done, G + 1)
                nc.gpsimd.tensor_tensor(z_sb[:, i, :, :], zt[:, i, :, 0:DH],
                                        recip[:, i, :].rearrange("p (c a) -> p c a", a=1).broadcast_to([P, DH, DH]),
                                        ALU.mult).then_inc(z_done, 1)
                pool.wait_ge(z_done, G + 1)
                y = normed[:, tile, :].rearrange("p (c d) -> p c d", d=DH)
                nc.gpsimd.tensor_tensor(y, y, z_sb[:, i, :, :], ALU.add).then_inc(y_done, 1)

            pool.wait_ge(xn_kept, B)
            pool.wait_ge(v_done, B)
            low_shift(0, 0)

            def phase2(b):
                for g in range(NG):
                    G = NG * b + g
                    if not (known(G) and G < 2):
                        pool.wait_ge(pv_done, G - 1)
                    nc.gpsimd.tensor_copy(v_aug[:, g % 2, :, :, 0:DH],
                                          v_all[:, b, :, HG * DH * g:HG * DH * (g + 1)].rearrange("p t (h d) -> p t h d", d=DH)
                                          ).then_inc(v_aug_done, 1)
                    if not (known(G) and G + 1 >= GALL):
                        low_shift(G + 1, (g + 1) % 2)
                    if not (known(G) and G < 2):
                        add_z(G - 2, G - 2, g % 2)

            for_batches(pool, phase2)
            add_z(GALL - 2, GALL - 2, 0)
            add_z(GALL - 1, GALL - 1, 1)

            def start_sum(T, j):
                pool.wait_ge(xf_done, T + 1)
                if not (known(T) and T < 2):
                    pool.wait_ge(sum_done, 3 * (T - 1))
                nc.gpsimd.tensor_tensor(even[j], x1[j], xf[j], ALU.add).then_inc(even_set, 1)

            def make_x1(T, j, p):
                pool.wait_ge(u_done, T + 1)
                nc.gpsimd.tensor_tensor(u[j], u[j], gamma_bc[:, :], ALU.mult).then_inc(u_gamma, 1)
                pool.wait_ge(u_gamma, T + 1)
                nc.gpsimd.tensor_tensor(u[j], u[j], beta_bc[:, :], ALU.add).then_inc(u_beta, 1)
                pool.wait_ge(u_beta, T + 1)
                pool.wait_ge(x_res_in[j], LOADS * (p + 1))
                if not (known(T) and T < 2):
                    pool.wait_ge(xf_done, T - 1)
                nc.gpsimd.tensor_tensor(x1[j], u[j], x_res[j], ALU.add).then_inc(x1_done, 1)

            def finish_sum(T, j, p):
                pool.wait_ge(mix_done, MIX * (T + 1))
                nc.gpsimd.tensor_tensor(even[j], even[j], odd[j], ALU.add).then_inc(sum_done, 1)
                for e in range(2):
                    pool.wait_ge(scaled_done, 2 * T + e + 1)
                    pool.wait_ge(sum_done, 3 * T + e + 1)
                    if e == 1 and not (known(T) and T < 2):
                        pool.wait_ge(out_stored[j], LOADS * p)
                    nc.gpsimd.tensor_tensor((even, result)[e][j], even[j], scaled[j][:, e, :], ALU.add).then_inc(sum_done, 1)

            make_x1(0, 0, 0)
            make_x1(1, 1, 0)
            start_sum(0, 0)
            make_x1(2, 0, 1)

            def phase3(p):
                for j in range(2):
                    T = 2 * p + j
                    if not (known(T) and T + 1 >= NT):
                        start_sum(T + 1, 1 - j)
                    if not (known(T) and T + 3 >= NT):
                        make_x1(T + 3, 1 - j, p + 1 + j)
                    finish_sum(T, j, p)

            phase3(0)
            with pool.Fori(1, NT // 2 - 2) as p:
                phase3(p)
            phase3(NT // 2 - 2)
            phase3(NT // 2 - 1)

        @block.scalar
        def _(act):
            act.wait_ge(consts_set, 5 + E)

            def take_std(n, j):
                act.wait_ge(var_done, n + 1)
                nc.scalar.activation(std[:, j, :], mv[:, j, :, 1], ACT.Sqrt, bias=eps[:, 0:1]).then_inc(std_done, 1)

            def high_and_mid(n, j, p, side, ready, bank, bias):
                act.wait_ge(ready, n + 1)
                if not (known(p) and p == 0):
                    act.wait_ge(op_stored[j], STORES * p)
                for m in range(KC):
                    nc.scalar.activation(parts[j][:, side, 0, m, :], ps[:, bank + m, :], ACT.Identity,
                                         bias=bias[:, m:m + 1]).then_inc(hi_done[side], 1)
                act.wait_ge(rest_done[side], KC * (n + 1))
                nc.scalar.activation(parts[j][:, side, 1, :, :], rest[:, side, :, :], ACT.Copy).then_inc(mid_done[side], 1)

            take_std(0, 0)
            act.wait_ge(consts_in, 9 * LOADS)

            def phase1(p, last):
                for j in range(2):
                    n = 2 * p + j
                    act.wait_ge(xT_ready, n + 1)
                    if not (known(p) and p == 0):
                        act.wait_ge(q_ready, n - 1)
                    nc.scalar.activation(xnT[j], ps[:, 0:KC, :], ACT.Copy).then_inc(xnT_done, 1)
                    high_and_mid(n, j, p, 1, k_ready, 4, bias_k)
                    if not (last and j == 1):
                        take_std(n + 1, 1 - j)
                    high_and_mid(n, j, p, 0, q_ready, 2, bias_q)

            phase1(0, False)
            with act.Fori(1, B // 2 - 1) as p:
                phase1(p, False)
            phase1(B // 2 - 1, True)

            for j in range(2):
                act.wait_ge(op_stored[j], STORES * (B // 2))
            act.wait_ge(xn_kept, B)

            def high_shift(G, i):
                act.wait_ge(maxT_ready, G + 1)
                if not (known(G) and G < 2):
                    act.wait_ge(sh_stored, LOADS * (G - 1))
                nc.scalar.activation(shift_parts[:, i, 0, :], maxT[:, i, :], ACT.Copy, scale=-1.0).then_inc(sh_hi, 1)
                nc.scalar.activation(shift[:, i, :], maxT[:, i, :], ACT.Copy, scale=-1.0).then_inc(shift_set, 1)

            def take_zT(G, i):
                act.wait_ge(pv_done, G + 1)
                if not (known(G) and G < 2):
                    act.wait_ge(zt_done, G - 1)
                nc.scalar.activation(zT[:, i, :], ps[:, ZT_BANK, :], ACT.Copy).then_inc(zT_done, 1)

            high_shift(0, 0)

            def phase2(b):
                for g in range(NG):
                    G = NG * b + g
                    for h in range(HG):
                        for kt in range(TT):
                            n = HG * TT * G + TT * h + kt
                            act.wait_ge(st_ready, n + 1)
                            if h == 0 and kt == 0 and not (known(G) and G < 2):
                                act.wait_ge(pv_done, G - 1)
                            nc.scalar.activation(probs[:, g % 2, h, kt, :], st_bank(TT * (HG * g + h) + kt), ACT.Exp).then_inc(exp_done, 1)
                            if h == 1 and kt == 0 and not (known(G) and G + 1 >= GALL):
                                high_shift(G + 1, (g + 1) % 2)
                    if not (known(G) and G < 1):
                        take_zT(G - 1, (g + 1) % 2)
                    if known(G) and G == GALL - 2:
                        act.wait_ge(experts_in, 2 * LOADS)
                        nc.scalar.activation(experts_hi[:, :, :], experts, ACT.Copy).then_inc(experts_cut, 1)

            for_batches(act, phase2)
            take_zT(GALL - 1, 1)

            def e_take_std(r):
                act.wait_ge(e_var, r + 1)
                if not (known(r) and r == 0):
                    act.wait_ge(e_rstd, r)
                nc.scalar.activation(std[:, 0, 0:2], mv[:, 0, 0:2, 1], ACT.Sqrt, bias=eps[:, 0:1]).then_inc(e_std, 1)

            def take_xfT(T, j):
                act.wait_ge(xfT_ready, T + 1)
                if not (known(T) and T < 2):
                    act.wait_ge(expert_ready, (E // 2) * (T - 1))
                nc.scalar.activation(xfT_hi[:, j, :, :], ps[:, 4, 0:D].rearrange("p (c s) -> p c s", c=KC), ACT.Copy).then_inc(xfT_high, 1)

            def scale_last(T, j):
                act.wait_ge(best_done, 4 * (T + 1))
                if not (known(T) and T < 2):
                    act.wait_ge(sum_done, 3 * (T - 1))
                act.wait_ge(expert_ready, (E // 2) * (T + 1))
                for e in range(2):
                    nc.scalar.activation(scaled[j][:, e, :], ps[:, E // 2 - 1, e * D:(e + 1) * D], ACT.Copy,
                                         scale=chosen[j][:, MIX + e:MIX + e + 1]).then_inc(scaled_done, 1)

            for r in range(3):
                e_take_std(r)
            take_xfT(0, 0)

            def phase3(p):
                for j in range(2):
                    T = 2 * p + j
                    if not (known(T) and T + 1 >= NT):
                        e_take_std(T + 3)
                        take_xfT(T + 1, 1 - j)
                    scale_last(T, j)

            phase3(0)
            with act.Fori(1, NT // 2 - 1) as p:
                phase3(p)
            phase3(NT // 2 - 1)

        @block.vector
        def _(dve):
            def norm_batch(n, j, p):
                dve.wait_ge(batch_in[j], 2 * LOADS * (p + 1))
                for t in range(TT):
                    nc.vector.bn_stats(bn[:, j, t, :], x_in[j][:, t, :]).then_inc(stats_step, 1)
                dve.wait_ge(stats_step, TT * (n + 1))
                carry_wait_dve()
                for t in range(TT):
                    ins = nc.vector.bn_aggr(mv[:, j, t, :], bn[:, j, t, :])
                ins.then_inc(var_done, 1)
                dve.wait_ge(std_done, n + 1)
                nc.vector.reciprocal(rstd[:, j, :], std[:, j, :]).then_inc(rstd_done, 1)
                dve.wait_ge(rstd_done, n + 1)
                dve.wait_ge(var_done, n + 1)
                if not (known(n) and n < 2):
                    dve.wait_ge(xT_ready, n - 1)
                    dve.wait_ge(xn_kept, n - 1)
                for t in range(TT):
                    ins = nc.vector.tensor_scalar(xn[j][:, t, :], x_in[j][:, t, :], mv[:, j, t, 0:1], rstd[:, j, t:t + 1],
                                                  ALU.subtract, ALU.mult)
                ins.then_inc(xn_done, 1)

            def take_rest(n, j, side, bank, bias):
                if not (known(n) and n == 0):
                    dve.wait_ge(lo_done[side], n)
                    dve.wait_ge(mid_done[side], n)
                for m in range(KC):
                    dve.wait_ge(hi_done[side], KC * n + m + 1)
                    nc.vector.scalar_tensor_tensor(rest[:, side, m, :], ps[:, bank + m, :], bias[:, m:m + 1],
                                                   parts[j][:, side, 0, m, :], ALU.add, ALU.subtract).then_inc(rest_done[side], 1)

            norm_batch(0, 0, 0)
            dve.wait_ge(consts_in, 9 * LOADS)

            def phase1(p, last):
                for j in range(2):
                    n = 2 * p + j
                    take_rest(n, j, 1, 4, bias_k)
                    dve.wait_ge(v_ready, n + 1)
                    for i in range(2):
                        ins = nc.vector.tensor_tensor(v_all[:, n, 2 * i:2 * i + 2, :],
                                                      ps[:, 6 + i, :].rearrange("p (t d) -> p t d", t=2),
                                                      bias_v[:, :].rearrange("p (a d) -> p a d", a=1).broadcast_to([P, 2, D]), ALU.add)
                    ins.then_inc(v_done, 1)
                    if not (last and j == 1):
                        norm_batch(n + 1, 1 - j, p + j)
                    take_rest(n, j, 0, 2, bias_q)

            phase1(0, False)
            with dve.Fori(1, B // 2 - 1) as p:
                phase1(p, False)
            phase1(B // 2 - 1, True)

            def row_maxima(G, i, unit):
                dve.wait_ge(scores_ready, 2 * HG * G + unit + 1)
                nc.vector.reduce_max(row_max[:, i, 2 * unit:2 * unit + 2], mx_bank(unit), AX_X).then_inc(max_done, 1)

            def transpose_max(G, i):
                dve.wait_ge(max_done, 2 * HG * (G + 1))
                if not (known(G) and G < 2):
                    dve.wait_ge(shift_set, G - 1)
                nc.vector.transpose(maxT[:, i, :], row_max[:, i, :]).then_inc(maxT_ready, 1)

            def token_major(G, i):
                dve.wait_ge(zT_done, G + 1)
                if not (known(G) and G < 2):
                    dve.wait_ge(z_done, G - 1)
                nc.vector.transpose(zt[:, i, :, :], zT[:, i, :].rearrange("p (a c) -> p c a", c=DH)).then_inc(zt_done, 1)
                dve.wait_ge(zt_done, G + 1)
                nc.vector.reciprocal(recip[:, i, :], zt[:, i, :, DH]).then_inc(recip_done, 1)

            dve.wait_ge(consts_set, 5 + E)
            for unit in range(2 * HG):
                row_maxima(0, 0, unit)
            transpose_max(0, 0)
            for unit in range(2 * HG):
                row_maxima(1, 1, unit)

            def phase2(b):
                for g in range(NG):
                    G = NG * b + g
                    for unit in range(2 * HG):
                        if not (known(G) and G + 2 >= GALL):
                            row_maxima(G + 2, g % 2, unit)
                        if unit == 0 and not (known(G) and G + 1 >= GALL):
                            transpose_max(G + 1, (g + 1) % 2)
                        if unit == 2 and not (known(G) and G < 2):
                            token_major(G - 2, g % 2)

            for_batches(dve, phase2)
            dve.wait_ge(experts_cut, 1)
            dve.wait_ge(v_aug_done, GALL)
            nc.vector.tensor_tensor(experts_lo[:, :, :], experts, experts_hi[:, :, :].bitcast(F32), ALU.subtract).then_inc(experts_ready, 1)
            token_major(GALL - 2, 0)
            token_major(GALL - 1, 1)

            def two_norms(r, a, b, between):
                todo = [(i, t) for i, t in ((0, a), (1, b)) if t is not None]
                src = {0: lambda T, j: normed[:, T, :], 1: lambda T, j: x1[j]}
                if b is not None:
                    dve.wait_ge(x1_done, b[0] + 1)
                for i, t in todo:
                    nc.vector.bn_stats(bn[:, 0, i, :], src[i](*t)).then_inc(e_stats, 1)
                between[0]()
                dve.wait_ge(e_stats, r + 1 if b is None else NT + r - 1 if a is None else 2 * r)
                carry_wait_dve()
                for i, t in todo:
                    ins = nc.vector.bn_aggr(mv[:, 0, i, :], bn[:, 0, i, :])
                ins.then_inc(e_var, 1)
                between[1]()
                dve.wait_ge(e_std, r + 1)
                nc.vector.reciprocal(rstd[:, 0, 0:2], std[:, 0, 0:2]).then_inc(e_rstd, 1)
                dve.wait_ge(e_rstd, r + 1)
                dve.wait_ge(e_var, r + 1)
                for i, t in reversed(todo):
                    T, j = t
                    if i == 0:
                        if not (known(T) and T < 2):
                            dve.wait_ge(x1_done, T - 1)
                    elif not (known(T) and T < 2):
                        dve.wait_ge(even_set, T - 1)
                        dve.wait_ge(xfT_ready, T - 1)
                    nc.vector.tensor_scalar((u, xf)[i][j], src[i](T, j), mv[:, 0, i, 0:1], rstd[:, 0, i:i + 1],
                                            ALU.subtract, ALU.mult).then_inc((u_done, xf_done)[i], 1)

            def choose(T, j, step):
                score = ps[:, 5, D - E:D]
                if step == 0:
                    dve.wait_ge(gate_ready, T + 1)
                    nc.vector.reduce_max(best, score, AX_X).then_inc(best_done, 1)
                elif step == 1:
                    dve.wait_ge(best_done, 4 * T + 1)
                    nc.vector.scalar_tensor_tensor(tied, score, best, rank_weight[:, :], ALU.is_equal, ALU.mult).then_inc(best_done, 1)
                elif step == 2:
                    dve.wait_ge(best_done, 4 * T + 2)
                    nc.vector.reduce_max(first, tied, AX_X).then_inc(best_done, 1)
                else:
                    if not (known(T) and T < 2):
                        dve.wait_ge(scaled_done, 2 * (T - 1))
                    dve.wait_ge(best_done, 4 * T + 3)
                    nc.vector.tensor_scalar(chosen[j], rank_weight[:, :], first, None, ALU.is_equal).then_inc(best_done, 1)

            def mix(T, j, e):
                if e == 0:
                    dve.wait_ge(best_done, 4 * T + 4)
                    dve.wait_ge(even_set, T + 1)
                if e % 2 == 0:
                    dve.wait_ge(expert_ready, (E // 2) * T + e // 2 + 1)
                if e >= 2:
                    dve.wait_ge(mix_done, MIX * T + e - 1)
                out_e = ps[:, e // 2, (e % 2) * D:(e % 2 + 1) * D]
                if e == 1:
                    if not (known(T) and T < 2):
                        dve.wait_ge(sum_done, 3 * (T - 1))
                    nc.vector.tensor_scalar(odd[j], out_e, chosen[j][:, e:e + 1], None, ALU.mult).then_inc(mix_done, 1)
                else:
                    total = (even, odd)[e % 2][j]
                    nc.vector.scalar_tensor_tensor(total, out_e, chosen[j][:, e:e + 1], total, ALU.mult, ALU.add).then_inc(mix_done, 1)

            def low_xfT(T, j):
                dve.wait_ge(xfT_high, T + 1)
                if not (known(T) and T < 2):
                    dve.wait_ge(expert_ready, (E // 2) * (T - 1))
                nc.vector.tensor_tensor(xfT_lo[:, j, :, :], ps[:, 4, 0:D].rearrange("p (c s) -> p c s", c=KC),
                                        xfT_hi[:, j, :, :].bitcast(F32), ALU.subtract).then_inc(xfT_low, 1)

            nothing = [lambda: None] * 2
            dve.wait_ge(y_done, GALL)
            dve.wait_ge(pv_done, GALL)
            two_norms(0, (0, 0), None, nothing)
            two_norms(1, (1, 1), None, nothing)
            two_norms(2, (2, 0), (0, 0), nothing)
            low_xfT(0, 0)

            def phase3(p):
                for j in range(2):
                    T = 2 * p + j

                    def early():
                        choose(T, j, 0)
                        choose(T, j, 1)

                    def middle():
                        choose(T, j, 2)
                        choose(T, j, 3)

                    def late():
                        mix(T, j, 0)
                        mix(T, j, 1)
                    if known(T) and T + 1 >= NT:
                        early(), middle(), late()
                        for e in range(2, MIX):
                            mix(T, j, e)
                    else:
                        a = None if known(T) and T + 3 >= NT else (T + 3, 1 - j)
                        two_norms(T + 3, a, (T + 1, 1 - j), [early, middle])
                        late()
                        low_xfT(T + 1, 1 - j)
                        mix(T, j, 2)
                        mix(T, j, 3)
                        mix(T, j, 4)
                        mix(T, j, 5)

            phase3(0)
            with dve.Fori(1, NT // 2 - 2) as p:
                phase3(p)
            phase3(NT // 2 - 2)
            phase3(NT // 2 - 1)

        @block.tensor
        def _(pe):
            pe.wait_ge(consts_in, 9 * LOADS)

            def phase1(p):
                for j in range(2):
                    n = 2 * p + j
                    first = known(n) and n == 0
                    pe.wait_ge(xn_done, n + 1)
                    if not first:
                        pe.wait_ge(xnT_done, n)
                    for t in range(TT):
                        for c in range(KC):
                            ins = nc.tensor.transpose(ps[:, c, t * P:(t + 1) * P], xn[j][:, t, c * P:(c + 1) * P], identity[:, :])
                    ins.then_inc(xT_ready, 1)
                    pe.wait_ge(batch_in[j], 2 * LOADS * (p + 1))
                    if not first:
                        pe.wait_ge(rest_done[1], KC * n)
                    for m in range(KC):
                        for c in range(KC):
                            ins = nc.tensor.matmul(ps[:, 4 + m, :], wk[:, c, m * P:(m + 1) * P], ctx_in[j][:, c, :],
                                                   start=(c == 0), stop=(c == KC - 1))
                    ins.then_inc(k_ready, 1)
                    if not first:
                        pe.wait_ge(v_done, n)
                    for t in range(TT):
                        for c in range(KC):
                            ins = nc.tensor.matmul(ps[:, 6 + t // 2, (t % 2) * D:(t % 2 + 1) * D],
                                                   ctx_in[j][:, c, t * P:(t + 1) * P], wv[:, c, :],
                                                   start=(c == 0), stop=(c == KC - 1))
                    ins.then_inc(v_ready, 1)
                    pe.wait_ge(xnT_done, n + 1)
                    if not first:
                        pe.wait_ge(rest_done[0], KC * n)
                    for m in range(KC):
                        for c in range(KC):
                            ins = nc.tensor.matmul(ps[:, 2 + m, :], wq[:, c, m * P:(m + 1) * P], xnT[j][:, c, :],
                                                   start=(c == 0), stop=(c == KC - 1))
                    ins.then_inc(q_ready, 1)

            phase1(0)
            with pe.Fori(1, B // 2) as p:
                phase1(p)
            pe.wait_ge(rest_done[0], KC * B)
            pe.wait_ge(rest_done[1], KC * B)
            pe.wait_ge(v_done, B)
            pe.wait_ge(xnT_done, B)
            pe.wait_ge(consts_set, 5 + E)

            def score(G, g, h, qt):
                unit = 2 * h + qt // 2
                if qt % 2 == 0:
                    if h == 0 and qt == 0:
                        b = G_batch(G)
                        pe.wait_ge(op_loaded[g], 2 * LOADS * (b + 1))
                    if not (known(G) and G == 0 and unit < 2):
                        pe.wait_ge(max_done, 2 * HG * G + unit - 1)
                hd = HG * g + h
                ins = nc.tensor.matmul(mx_bank(unit)[:, qt % 2, :], q_op[0:ROWS, hd, qt * P:(qt + 1) * P], k_op[0:ROWS, hd, :],
                                       start=True, stop=True)
                if qt % 2:
                    ins.then_inc(scores_ready, 1)

            def shifted(G, g, h, kt):
                n = TT * (HG * g + h) + kt
                if h == 0 and kt == 0:
                    pe.wait_ge(sh_loaded[g % 2], 3 * LOADS * G_pair(G))
                if not (known(G) and TT * HG * G + TT * h + kt < 3):
                    pe.wait_ge(exp_done, ST_BATCH * G_batch(G) + st_before(n))
                hd = HG * g + h
                nc.tensor.matmul(st_bank(n), k_op[0:SROWS, hd, kt * P:(kt + 1) * P], q_op[0:SROWS, hd, :],
                                 start=True, stop=True).then_inc(st_ready, 1)

            def attend(G, i, kt):
                if kt == 0:
                    pe.wait_ge(v_aug_done, G + 1)
                    if not (known(G) and G == 0):
                        pe.wait_ge(zT_done, G)
                pe.wait_ge(exp_done, HG * TT * G + (HG - 1) * TT + kt + 1)
                for h in range(HG):
                    ins = nc.tensor.matmul(ps[2 * DH * h:2 * DH * (h + 1), ZT_BANK, :], v_aug[:, i, kt, h, :],
                                           probs[:, i, h, kt, :], start=(kt == 0), stop=(kt == TT - 1),
                                           tile_position=(0, 2 * DH * h))
                if kt == TT - 1:
                    ins.then_inc(pv_done, 1)

            batch_of = {}

            def G_batch(G):
                return G // NG if known(G) else batch_of["b"]

            def G_pair(G):
                return G // 2 + 1 if known(G) else 2 * batch_of["b"] + batch_of["g"] // 2 + 1

            def score_unit(G, g, h, half):
                for qt in (2 * half, 2 * half + 1):
                    score(G, g, h, qt)

            for h in range(HG):
                for half in range(2):
                    score_unit(0, 0, h, half)
            for h in range(HG):
                for half in range(2):
                    score_unit(1, 1, h, half)

            def phase2(b):
                for g in range(NG):
                    G = NG * b + g

                    def mx(h, half, second):
                        if not (known(G) and G + 2 >= GALL):
                            batch_of["b"] = b + (g + 2) // NG
                            score(G + 2, (g + 2) % NG, h, 2 * half + second)

                    def st(h, kt):
                        batch_of["b"], batch_of["g"] = b, g
                        shifted(G, g, h, kt)

                    for h in range(HG):
                        st(h, 0)
                        mx(h, 0, 0)
                        st(h, 1)
                        mx(h, 0, 1)
                        st(h, 2)
                        if not (known(G) and G == 0):
                            attend(G - 1, (g + 1) % 2, h)
                        mx(h, 1, 0)
                        st(h, 3)
                        mx(h, 1, 1)

            for_batches(pe, phase2)
            for kt in range(TT):
                attend(GALL - 1, 1, kt)

            def transpose_xf(T, j):
                pe.wait_ge(xf_done, T + 1)
                if not (known(T) and T == 0):
                    pe.wait_ge(xfT_low, T)
                for c in range(KC):
                    ins = nc.tensor.transpose(ps[:, 4, c * P:(c + 1) * P], xf[j][:, c * P:(c + 1) * P], identity[:, :])
                ins.then_inc(xfT_ready, 1)

            def halves(T, j, dst, cols):
                passes = [(l, r, c) for c in range(KC) for l, r in ((xfT_hi, experts_hi), (xfT_lo, experts_hi), (xfT_hi, experts_lo))]
                for n, (l, r, c) in enumerate(passes):
                    ins = nc.tensor.matmul(dst, l[:, j, c, :], r[:, c, cols], start=(n == 0), stop=(n == len(passes) - 1))
                return ins

            def gates(T, j):
                pe.wait_ge(xfT_high, T + 1)
                pe.wait_ge(xfT_low, T + 1)
                if not (known(T) and T == 0):
                    pe.wait_ge(best_done, 4 * T)
                halves(T, j, ps[:, 5, 0:D], slice(NE - D, NE)).then_inc(gate_ready, 1)

            def expert_pair(T, j, i):
                if not (known(T) and T == 0):
                    if i < MIX // 2:
                        pe.wait_ge(mix_done, MIX * (T - 1) + 2 * i + 2)
                    else:
                        pe.wait_ge(scaled_done, 2 * T)
                halves(T, j, ps[:, i, :], slice(2 * D * i, 2 * D * (i + 1))).then_inc(expert_ready, 1)

            pe.wait_ge(experts_ready, 1)
            pe.wait_ge(experts_cut, 1)
            pe.wait_ge(exp_done, HG * TT * GALL)
            pe.wait_ge(max_done, 2 * HG * GALL)
            transpose_xf(0, 0)
            gates(0, 0)

            def phase3(p):
                for j in range(2):
                    T = 2 * p + j
                    more = not (known(T) and T + 1 >= NT)
                    for i in range(E // 2):
                        expert_pair(T, j, i)
                        if i == 1 and more:
                            transpose_xf(T + 1, 1 - j)
                    if more:
                        gates(T + 1, 1 - j)

            phase3(0)
            with pe.Fori(1, NT // 2 - 1) as p:
                phase3(p)
            phase3(NT // 2 - 1)


def kernel(x, ctx_1024, L0_xattn_Wq, L0_xattn_bq, L0_xattn_Wk, L0_xattn_bk, L0_xattn_Wv, L0_xattn_bv,
           L0_xattn_gamma, L0_xattn_beta, L0_ffn_gate_w, L0_ffn_expert_w):
    import numpy as np
    import concourse.bacc as bacc
    from concourse.bass_utils import run_bass_kernel_spmd

    D = x.shape[-1]
    dh = D // H
    half = P // dh
    order = np.array([(m * half + p % half) * dh + p // half for m in range(D // P) for p in range(P)])
    c = np.ascontiguousarray
    arrays = {
        "x": c(x),
        "ctxT": c(np.transpose(np.asarray(ctx_1024), (0, 2, 1))),
        "WqT": c(np.asarray(L0_xattn_Wq)[order].T),
        "bq": c(np.asarray(L0_xattn_bq)[order].reshape(D // P, P).T),
        "WkT": c(np.asarray(L0_xattn_Wk)[order].T),
        "bk": c(np.asarray(L0_xattn_bk)[order].reshape(D // P, P).T),
        "WvT": c(np.asarray(L0_xattn_Wv).T),
        "bv": c(L0_xattn_bv),
        "gamma": c(L0_xattn_gamma),
        "beta": c(L0_xattn_beta),
        "gateT": c(np.asarray(L0_ffn_gate_w).T),
        "expertT": c(np.transpose(np.asarray(L0_ffn_expert_w), (2, 0, 1)).reshape(D, -1)),
        "identity_in": np.eye(P, dtype=np.float32),
    }
    nc = bacc.Bacc("TRN2", target_bir_lowering=False, num_devices=1)
    args = [nc.dram_tensor(f"in_{k}", a.shape, mybir.dt.from_np(a.dtype), kind="ExternalInput").ap() for k, a in arrays.items()]
    out = nc.dram_tensor("out_0", x.shape, F32, kind="ExternalOutput").ap()
    xattn_ffn_kernel(nc, *args, out)
    r = run_bass_kernel_spmd(nc, [{f"in_{k}": a for k, a in arrays.items()}], core_ids=[0])
    return r.results[0]["out_0"]
```

```python
from contextlib import ExitStack

import concourse.bass as bass
from concourse import mybir

P = 128
F32 = mybir.dt.float32
F32R = mybir.dt.float32r
BF16 = mybir.dt.bfloat16
ALU = mybir.AluOpType
ACT = mybir.ActivationFunctionType
AX_X = mybir.AxisListType.X

H = 16
EPS = 1e-5
Q_STORED, Q_PAIRS = (1, 0, 2), (0, 0, 1)
K_STORED, K_PAIRS = (2, 0, 1, 0), (1, 2, 0)
Q_BLOCKS, K_BLOCKS = [[stored[start + i] for start in pairs for i in range(2)]
                      for stored, pairs in ((Q_STORED, Q_PAIRS), (K_STORED, K_PAIRS))]
assert sorted(zip(Q_BLOCKS, K_BLOCKS)) == [(0, 0), (0, 1), (0, 2), (1, 0), (1, 1), (2, 0)]
NBLK = len(Q_BLOCKS)


def xattn_ffn_kernel(nc: bass.Bass, x, ctxT, WqT, bq, WkT, bk, WvT, bv, gamma, beta, gateT, expertT, identity_in, out):
    B, S, D = x.shape
    DH = D // H
    TT = S // P
    KC = D // P
    E = gateT.shape[1]
    HG = 4
    NG = H // HG
    GALL = B * NG
    HH = H // KC
    ROWS = NBLK * DH
    SROWS = ROWS + 3
    NT = B * TT
    LOADS = 16

    with ExitStack() as ctx:
        def sb(name, shape, dt=F32):
            return ctx.enter_context(nc.sbuf_tensor(name, shape, dt))

        def sem(name):
            return ctx.enter_context(nc.semaphore(name))

        identity = sb("identity", [P, P])
        w_offset = nc.sbuf_base + (-nc.sbuf_base) % 32
        weights = sb("weights", [P, 3, KC, D])
        wk, wv, wq = [weights[:, i] for i in range(3)]
        bias_q = sb("bias_q", [P, KC])
        bias_k = sb("bias_k", [P, KC])
        bias_v = sb("bias_v", [P, D])
        gamma_bc = sb("gamma_bc", [P, D])
        beta_bc = sb("beta_bc", [P, D])
        tiny = sb("tiny", [P, 1])
        zeros = sb("zeros", [P, 32])
        eps = sb("eps", [P, 1])
        rank_weight = sb("rank_weight", [P, E])
        normed = sb("normed", [P, NT, D])
        NE = E * D
        v_offset = nc.sbuf_base + (-nc.sbuf_base) % 32
        v_flat = sb("v_all", [P, 2 * KC * NE])
        v_all = v_flat[:, 0:B * TT * D].rearrange("p (b t d) -> p b t d", b=B, t=TT)
        experts = v_flat[:, 0:KC * NE].rearrange("p (c n) -> p c n", c=KC)
        gate = sb("gate", [P, KC, E])
        experts_hi = sb("experts_hi", [P, KC, NE], F32R)
        experts_lo = nc.alloc_sbuf_tensor_at("experts_lo", [P, KC, NE], F32R,
                                             offset=v_offset + 4 * KC * NE)
        xfT_hi = sb("xfT_hi", [P, 2, KC, P], F32R)
        xfT_lo = sb("xfT_lo", [P, 2, KC, P], F32R)
        work_offset = nc.sbuf_base + (-nc.sbuf_base) % 32
        work = sb("work", [P, 16384])
        q_op = sb("q_op", [P, H, S], BF16)
        k_op = sb("k_op", [P, H, S], BF16)
        v_aug = sb("v_aug", [P, 2, TT, HG, 2 * DH])
        zT = sb("zT", [P, 2, S])
        zt = sb("zt", [P, 2, DH, 2 * DH])
        z_sb = sb("z_sb", [P, 2, DH, DH])
        row_max = sb("row_max", [P, 2, 32])
        maxT = sb("maxT", [P, 2, 32])
        shift = sb("shift", [P, 2, 32])
        recip = sb("recip", [P, 2, DH])
        shift_parts = sb("shift_parts", [P, 2, 3, 32], BF16)
        shift_rest = sb("shift_rest", [P, 2, 32])
        bn = sb("bn", [P, 2, TT, 6])
        mv = sb("mv", [P, 2, TT, 2])
        std = sb("std", [P, 2, TT])
        rstd = sb("rstd", [P, 2, TT])
        ps = ctx.enter_context(nc.psum_tensor("ps", [P, 8, 512], F32))

        off = [0]

        def take(n):
            off[0] += n
            return work[:, off[0] - n:off[0]]

        x_in = [take(TT * D).rearrange("p (t d) -> p t d", t=TT) for _ in range(2)]
        ctx_in = [take(KC * S).rearrange("p (c s) -> p c s", c=KC) for _ in range(2)]

        def over_work(name, shape):
            n = shape[0] * shape[1]
            take(n)
            return nc.alloc_sbuf_tensor_at(name, [P] + shape, F32R, offset=work_offset + 4 * (off[0] - n))[:, :, :]
        xnT_hi = over_work("xnT_hi", [KC, S])
        xnT_lo = over_work("xnT_lo", [KC, S])
        wk_hi, wv_hi = [t[:, :, :, :].rearrange("p j c s -> p (j c s)").rearrange("p (c o) -> p c o", c=KC) for t in (xfT_hi, xfT_lo)]
        wq_hi = over_work("wq_hi", [KC, D])
        xn = [take(TT * D).rearrange("p (t d) -> p t d", t=TT),
              zT[:, :, :].rearrange("p j (a d) -> p (j a) d", d=D)]
        wk_lo, wv_lo, wq_lo = [
            nc.alloc_sbuf_tensor_at(name, [P, KC, D], F32R, offset=w_offset + 4 * KC * D * i)[:, :, :]
            for i, name in enumerate(("wk_lo", "wv_lo", "wq_lo"))]
        ctx_halves = experts_hi[:, :, :].rearrange("p c n -> p (c n)")[:, 0:4 * KC * S].rearrange(
            "p (i j c s) -> p i j c s", i=2, j=2, c=KC)
        ctx_hi = [ctx_halves[:, 0, j] for j in range(2)]
        ctx_lo = [ctx_halves[:, 1, j] for j in range(2)]
        off[0] = 8192
        parts = [take(2 * 3 * KC * S // 2).bitcast(BF16).rearrange("p (q a m s) -> p q a m s", q=2, a=3, m=KC)
                 for _ in range(2)]
        rest = take(2 * KC * S).rearrange("p (q m s) -> p q m s", q=2, m=KC)
        probs = work[:, :].rearrange("p (g h k q) -> p g h k q", g=2, h=HG, k=TT)
        q_free, k_free = [t[:, 0:2 * HG, :].rearrange("p h s -> p (h s)").bitcast(F32) for t in (q_op, k_op)]
        x_res = [q_free[:, i * D:(i + 1) * D] for i in (0, 1)]
        u = [q_free[:, i * D:(i + 1) * D] for i in (2, 3)]
        x1 = [q_free[:, i * D:(i + 1) * D] for i in (4, 5)]
        xf = [q_free[:, i * D:(i + 1) * D] for i in (6, 7)]
        even = [k_free[:, i * D:(i + 1) * D] for i in (0, 1)]
        odd = [k_free[:, i * D:(i + 1) * D] for i in (2, 3)]
        result = [k_free[:, i * D:(i + 1) * D] for i in (4, 5)]
        smalls = k_free[:, 6 * D:7 * D]
        xfT = [work[:, (4 + i * KC) * D:(4 + i * KC) * D + KC * P].rearrange("p (c s) -> p c s", c=KC) for i in range(2)]
        scaled = [work[:, i * D:(i + 2) * D].rearrange("p (e d) -> p e d", e=2) for i in (0, 2)]
        best = smalls[:, 0:1]
        tied = smalls[:, 8:8 + E]
        first = smalls[:, 16:17]
        chosen = [smalls[:, i:i + E] for i in (24, 32)]

        op_scr = nc.dram_tensor("op_scr", [B, 2, KC, len(K_STORED) * DH, HH * S], BF16, kind="Internal").ap()
        sh_scr = nc.dram_tensor("sh_scr", [2, 3, P, 32], BF16, kind="Internal").ap()

        x_b = x.rearrange("b (t p) d -> b p t d", p=P)
        ctxT_b = ctxT.rearrange("b (c p) s -> b p c s", p=P)
        x_t = x.rearrange("b (t p) d -> (b t) p d", p=P)
        out_t = out.rearrange("b (t p) d -> (b t) p d", p=P)

        wk_in = sem("wk_in")
        wv_in = sem("wv_in")
        wq_in = sem("wq_in")
        identity_loaded = sem("identity_loaded")
        bias_k_in = sem("bias_k_in")
        bias_q_in = sem("bias_q_in")
        bias_v_in = sem("bias_v_in")
        affine_in = sem("affine_in")
        gate_in = sem("gate_in")
        w_high = sem("w_high")
        w_low = sem("w_low")
        consts_set = sem("consts_set")
        ones_set = sem("ones_set")
        x_loaded = [sem(f"x_loaded{j}") for j in range(2)]
        ctx_loaded = [sem(f"ctx_loaded{j}") for j in range(2)]
        ctx_high = sem("ctx_high")
        ctx_low = sem("ctx_low")
        var_done = sem("var_done")
        stats_step = sem("stats_step")
        std_done = sem("std_done")
        rstd_done = sem("rstd_done")
        xn_done = sem("xn_done")
        xn_kept = sem("xn_kept")
        xT_ready = sem("xT_ready")
        xnT_high = sem("xnT_high")
        xnT_low = sem("xnT_low")
        k_ready = sem("k_ready")
        v_ready = sem("v_ready")
        q_ready = sem("q_ready")
        hi_done = [sem("hi_q"), sem("hi_k")]
        rest_done = [sem("rest_q"), sem("rest_k")]
        last_copied = [sem("last_copied_q"), sem("last_copied_k")]
        mid_done = [sem("mid_q"), sem("mid_k")]
        lo_done = [sem("lo_q"), sem("lo_k")]
        v_done = sem("v_done")
        last_v_done = sem("last_v_done")
        op_stored = [[sem(f"{s}_stored{j}") for j in range(2)] for s in "qk"]
        STORES = (len(Q_STORED) * LOADS, len(K_STORED) * LOADS)
        op_loaded = [sem(f"op_loaded{g}") for g in range(NG)]
        OP_LOADS = (len(Q_PAIRS) + len(K_PAIRS)) * LOADS
        scores_ready = sem("scores_ready")
        max_done = sem("max_done")
        maxT_ready = sem("maxT_ready")
        shift_set = sem("shift_set")
        sh_hi = sem("sh_hi")
        sh_rest = sem("sh_rest")
        sh_mid = sem("sh_mid")
        sh_lo = sem("sh_lo")
        sh_stored = sem("sh_stored")
        sh_loaded = [sem(f"sh_loaded{j}") for j in range(2)]
        st_ready = sem("st_ready")
        exp_done = sem("exp_done")
        v_aug_done = sem("v_aug_done")
        pv_done = sem("pv_done")
        zT_done = sem("zT_done")
        zt_done = sem("zt_done")
        recip_done = sem("recip_done")
        z_done = sem("z_done")
        y_done = sem("y_done")
        experts_in = sem("experts_in")
        x_res_in = [sem(f"x_res_in{j}") for j in range(2)]
        experts_cut = sem("experts_cut")
        experts_ready = sem("experts_ready")
        e_stats = sem("e_stats")
        e_var = sem("e_var")
        e_std = sem("e_std")
        e_rstd = sem("e_rstd")
        u_done = sem("u_done")
        u_gamma = sem("u_gamma")
        u_beta = sem("u_beta")
        x1_done = sem("x1_done")
        xf_done = sem("xf_done")
        even_set = sem("even_set")
        xfT_ready = sem("xfT_ready")
        xfT_high = sem("xfT_high")
        xfT_whole = sem("xfT_whole")
        xfT_low = sem("xfT_low")
        gate_ready = sem("gate_ready")
        best_done = sem("best_done")
        expert_ready = sem("expert_ready")
        mix_done = sem("mix_done")
        scaled_done = sem("scaled_done")
        last_sum_done = sem("last_sum_done")
        sum_done = sem("sum_done")
        out_stored = [sem(f"out_stored{j}") for j in range(2)]
        EARLY = 3
        MIX = E - 2

        block = ctx.enter_context(nc.Block())

        def carry_wait_dve():
            nc.vector.memset(tiny[:, 0:1], 0.0)

        def known(v):
            return isinstance(v, int)

        ST_BANKS = (0, 1, 7)
        ST_BATCH = NG * HG * TT

        def st_bank(n):
            return ps[:, ST_BANKS[n % 3], :]

        def st_before(n):
            return n - 2 if n >= 3 else max(m for m in range(-ST_BATCH, 0) if (m + ST_BATCH) % 3 == n % 3) + 1

        def mx_bank(G, n):
            if known(G) and G == 0:
                first = 2 if n == 0 or n % 2 else 0
            else:
                first = 4 - 2 * (n % 2)
            return ps[:, first:first + 2, :]
        ZT_BANK = 6

        def for_batches(eng, body):
            body(0)
            with eng.Fori(1, B - 1) as b:
                body(b)
            body(B - 1)

        @block.sync
        def _(sp):
            def load_x(n, j):
                sp.dma_start(x_in[j], x_b[n]).then_inc(x_loaded[j], LOADS)

            def load_ctx(n, j):
                sp.dma_start(ctx_in[j], ctxT_b[n]).then_inc(ctx_loaded[j], LOADS)

            def over_rows(vector):
                return vector.rearrange("(a d) -> a d", a=1).broadcast_to([P, D])

            sp.dma_start(wk, WkT.rearrange("(c p) o -> p c o", p=P)).then_inc(wk_in, LOADS)
            load_ctx(0, 0)
            load_x(0, 0)
            sp.dma_start(identity[:, :], identity_in).then_inc(identity_loaded, LOADS)
            sp.dma_start(bias_k[:, :], bk).then_inc(bias_k_in, LOADS)
            sp.dma_start(wv, WvT.rearrange("(c p) o -> p c o", p=P)).then_inc(wv_in, LOADS)
            sp.dma_start(bias_v[:, :], over_rows(bv)).then_inc(bias_v_in, LOADS)
            sp.dma_start(wq, WqT.rearrange("(c p) o -> p c o", p=P)).then_inc(wq_in, LOADS)
            sp.dma_start(bias_q[:, :], bq).then_inc(bias_q_in, LOADS)
            load_ctx(1, 1)
            load_x(1, 1)
            sp.dma_start(gate[:, :, :], gateT.rearrange("(c p) e -> p c e", p=P)).then_inc(gate_in, LOADS)
            sp.dma_start(gamma_bc[:, :], over_rows(gamma)).then_inc(affine_in, LOADS)
            sp.dma_start(beta_bc[:, :], over_rows(beta)).then_inc(affine_in, LOADS)

            def store_parts(n, j, side):
                sp.wait_ge(lo_done[side], n + 1)
                sp.wait_ge(mid_done[side], n + 1)
                for i, part in reversed(list(enumerate((Q_STORED, K_STORED)[side]))):
                    sp.dma_start(op_scr[n, side, :, DH * i:DH * (i + 1), :].rearrange("m r (h s) -> (r h) m s", s=S),
                                 parts[j][:, side, part, :, :]).then_inc(op_stored[side][j], LOADS)

            def phase1(p):
                for j in range(2):
                    n = 2 * p + j
                    if not (known(n) and n + 2 >= B):
                        sp.wait_ge(ctx_high, n + 1)
                        sp.wait_ge(ctx_low, n + 1)
                        load_ctx(n + 2, j)
                        sp.wait_ge(xn_done, n + 1)
                        load_x(n + 2, j)
                    if not (known(n) and n == 0):
                        store_parts(n - 1, 1 - j, 0)
                    store_parts(n, j, 1)
                    if known(n) and n == B - 2:
                        load_op(0, 1)

            def load_op(b, g):
                m, h0 = g * HG // HH, g * HG % HH
                for side, dst, pairs in ((0, q_op, Q_PAIRS), (1, k_op, K_PAIRS)):
                    for i, start in enumerate(pairs):
                        sp.dma_start(dst[2 * DH * i:2 * DH * (i + 1), HG * g:HG * (g + 1), :],
                                     op_scr[b, side, m, DH * start:DH * (start + 2), h0 * S:(h0 + HG) * S].rearrange(
                                         "r (h s) -> r h s", s=S)).then_inc(op_loaded[g], LOADS)

            def store_shift(G, g):
                sp.wait_ge(sh_lo, G + 1)
                sp.wait_ge(sh_hi, G + 1)
                sp.dma_start(sh_scr[g % 2].rearrange("a p q -> p a q"), shift_parts[:, g % 2, :, :]).then_inc(sh_stored, LOADS)

            def fetch_shift(G, g):
                sp.wait_ge(sh_stored, LOADS * (G + 1))
                for part in range(3):
                    sp.dma_start(q_op[ROWS + part:ROWS + part + 1, HG * g:HG * (g + 1), :].rearrange(
                                     "x h (t a r) -> x (h t) a r", a=4, r=32),
                                 sh_scr[g % 2, part:part + 1].rearrange("x (a c) r -> x c a r", a=4)[:, 0:HG * TT, :, :]
                                 ).then_inc(sh_loaded[g % 2], LOADS)

            phase1(0)
            with sp.Fori(1, B // 2 - 1) as p:
                phase1(p)
            for side in range(2):
                sp.wait_ge(op_stored[side][0], STORES[side])
            load_op(0, 0)
            phase1(B // 2 - 1)
            store_shift(0, 0)
            load_op(0, 2)
            fetch_shift(0, 0)
            store_parts(B - 1, 1, 0)
            load_op(0, 3)

            def phase2(b):
                if known(b) and b == B - 1:
                    sp.wait_ge(v_aug_done, NG * (B - 1))
                    sp.dma_start(experts, expertT.rearrange("(c p) n -> p c n", p=P)).then_inc(experts_in, LOADS)
                for g in range(NG):
                    G = NG * b + g
                    if known(G) and G == 0:
                        store_shift(1, 1)
                        fetch_shift(1, 1)
                        for side in range(2):
                            for j in range(2):
                                sp.wait_ge(op_stored[side][j], STORES[side] * (B // 2))
                        continue
                    if not (known(G) and G + 3 >= GALL):
                        sp.wait_ge(st_ready, HG * TT * G)
                        load_op(b + (g + 3) // NG, (g + 3) % NG)
                    if not (known(G) and G + 1 >= GALL):
                        store_shift(G + 1, (g + 1) % NG)
                        fetch_shift(G + 1, (g + 1) % NG)

            for_batches(sp, phase2)

            sp.wait_ge(st_ready, HG * TT * (GALL - 2))
            for j in range(2):
                sp.dma_start(x_res[j], x_t[j]).then_inc(x_res_in[j], LOADS)

            for j in range(2):
                sp.wait_ge(x1_done, j + 1)
                sp.dma_start(x_res[j], x_t[2 + j]).then_inc(x_res_in[j], LOADS)

            def phase3(pair, last):
                for j in range(2):
                    T = 2 * pair + j
                    if not last:
                        sp.wait_ge(x1_done, T + 3)
                        sp.dma_start(x_res[j], x_t[T + 4]).then_inc(x_res_in[j], LOADS)
                    if known(T) and T == NT - 1:
                        sp.wait_ge(last_sum_done, 1)
                    else:
                        sp.wait_ge(sum_done, 3 * (T + 1))
                    sp.dma_start(out_t[T], result[j]).then_inc(out_stored[j], LOADS)

            with sp.Fori(0, NT // 2 - 2) as pair:
                phase3(pair, False)
            phase3(NT // 2 - 2, True)
            phase3(NT // 2 - 1, True)
            for j in range(2):
                sp.wait_ge(out_stored[j], LOADS * (NT // 2))

        @block.gpsimd
        def _(pool):
            nc.gpsimd.memset(eps[:, :], EPS).then_inc(consts_set, 1)
            nc.gpsimd.memset(zeros[:, :], 0.0).then_inc(consts_set, 1)
            nc.gpsimd.memset(row_max[:, :, :], 0.0).then_inc(consts_set, 1)
            nc.gpsimd.memset(v_aug[:, :, :, :, :], 1.0).then_inc(consts_set, 1)
            for e in range(E):
                nc.gpsimd.memset(rank_weight[:, e:e + 1], float(E - e)).then_inc(consts_set, 1)

            pool.wait_ge(consts_set, 4 + E)

            def low_ctx(n, j, p):
                pool.wait_ge(ctx_loaded[j], LOADS * (p + 1))
                pool.wait_ge(ctx_high, n + 1)
                if not (known(n) and n < 2):
                    pool.wait_ge(v_ready, n - 1)
                nc.gpsimd.tensor_tensor(ctx_lo[j], ctx_in[j], ctx_hi[j].bitcast(F32), ALU.subtract).then_inc(ctx_low, 1)

            def low_shift(G, i):
                pool.wait_ge(sh_hi, G + 1)
                pool.wait_ge(shift_set, G + 1)
                nc.gpsimd.tensor_tensor(shift_rest[:, i, :], shift[:, i, :], shift_parts[:, i, 0, :],
                                        ALU.subtract).then_inc(sh_rest, 1)
                pool.wait_ge(sh_rest, G + 1)
                nc.gpsimd.tensor_tensor(shift_parts[:, i, 1, :], shift_rest[:, i, :], zeros[:, :], ALU.add).then_inc(sh_mid, 1)
                pool.wait_ge(sh_mid, G + 1)
                nc.gpsimd.tensor_tensor(shift_parts[:, i, 2, :], shift_rest[:, i, :], shift_parts[:, i, 1, :],
                                        ALU.subtract).then_inc(sh_lo, 1)

            def last_rest(side):
                pool.wait_ge(last_copied[side], KC)
                pool.wait_ge(hi_done[side], KC * B)
                nc.gpsimd.tensor_tensor(rest[:, side, :, :], rest[:, side, :, :], parts[1][:, side, 0, :, :],
                                        ALU.subtract).then_inc(rest_done[side], KC)

            def low_part(n, j, side):
                pool.wait_ge(mid_done[side], n + 1)
                pool.wait_ge(rest_done[side], KC * (n + 1))
                nc.gpsimd.tensor_tensor(parts[j][:, side, 2, :, :], rest[:, side, :, :], parts[j][:, side, 1, :, :],
                                        ALU.subtract).then_inc(lo_done[side], 1)

            pool.wait_ge(consts_set, 4 + E)
            for g in range(NG):
                nc.gpsimd.memset(k_op[ROWS:P, HG * g:HG * (g + 1), :], 1.0).then_inc(ones_set, 1)
            pool.wait_ge(ones_set, NG)

            def phase1(p):
                for j in range(2):
                    n = 2 * p + j
                    if not (known(n) and n + 1 >= B):
                        low_ctx(n + 1, 1 - j, p + j)
                    if not (known(n) and n == 0):
                        low_part(n - 1, 1 - j, 0)
                    if known(n) and n == B - 1:
                        last_rest(1)
                    low_part(n, j, 1)

            phase1(0)
            with pool.Fori(1, B // 2 - 1) as p:
                phase1(p)
            phase1(B // 2 - 1)
            low_shift(0, 0)
            last_rest(0)
            low_part(B - 1, 1, 0)
            pool.wait_ge(bias_v_in, LOADS)
            pool.wait_ge(v_done, B)
            nc.gpsimd.tensor_tensor(v_all[:, B - 1, :, :], v_all[:, B - 1, :, :],
                                    bias_v[:, :].rearrange("p (a d) -> p a d", a=1).broadcast_to([P, TT, D]), ALU.add).then_inc(last_v_done, 1)
            pool.wait_ge(last_v_done, 1)
            pool.wait_ge(xn_kept, B)

            def add_z(G, tile, i):
                pool.wait_ge(recip_done, G + 1)
                nc.gpsimd.tensor_tensor(z_sb[:, i, :, :], zt[:, i, :, 0:DH],
                                        recip[:, i, :].rearrange("p (c a) -> p c a", a=1).broadcast_to([P, DH, DH]),
                                        ALU.mult).then_inc(z_done, 1)
                pool.wait_ge(z_done, G + 1)
                y = normed[:, tile, :].rearrange("p (c d) -> p c d", d=DH)
                nc.gpsimd.tensor_tensor(y, y, z_sb[:, i, :, :], ALU.add).then_inc(y_done, 1)

            def phase2(b):
                for g in range(NG):
                    G = NG * b + g
                    if not (known(G) and G < 2):
                        pool.wait_ge(pv_done, G - 1)
                    nc.gpsimd.tensor_copy(v_aug[:, g % 2, :, :, 0:DH],
                                          v_all[:, b, :, HG * DH * g:HG * DH * (g + 1)].rearrange("p t (h d) -> p t h d", d=DH)
                                          ).then_inc(v_aug_done, 1)
                    if not (known(G) and G + 1 >= GALL):
                        low_shift(G + 1, (g + 1) % 2)
                    if not (known(G) and G < 2):
                        add_z(G - 2, G - 2, g % 2)

            for_batches(pool, phase2)

            def start_sum(T, j):
                pool.wait_ge(xf_done, T + 1)
                if not (known(T) and T < 2):
                    pool.wait_ge(sum_done, 3 * (T - 1))
                nc.gpsimd.tensor_tensor(even[j], x1[j], xf[j], ALU.add).then_inc(even_set, 1)

            def make_x1(T, j, p):
                pool.wait_ge(u_done, T + 1)
                nc.gpsimd.tensor_tensor(u[j], u[j], gamma_bc[:, :], ALU.mult).then_inc(u_gamma, 1)
                pool.wait_ge(u_gamma, T + 1)
                nc.gpsimd.tensor_tensor(u[j], u[j], beta_bc[:, :], ALU.add).then_inc(u_beta, 1)
                pool.wait_ge(u_beta, T + 1)
                pool.wait_ge(x_res_in[j], LOADS * (p + 1))
                if not (known(T) and T < 2):
                    pool.wait_ge(xf_done, T - 1)
                nc.gpsimd.tensor_tensor(x1[j], u[j], x_res[j], ALU.add).then_inc(x1_done, 1)

            def finish_sum(T, j, p):
                pool.wait_ge(mix_done, MIX * (T + 1))
                nc.gpsimd.tensor_tensor(even[j], even[j], odd[j], ALU.add).then_inc(sum_done, 1)
                for e in range(2):
                    pool.wait_ge(scaled_done, 2 * T + e + 1)
                    pool.wait_ge(sum_done, 3 * T + e + 1)
                    if e == 1 and not (known(T) and T < 2):
                        pool.wait_ge(out_stored[j], LOADS * p)
                    nc.gpsimd.tensor_tensor((even, result)[e][j], even[j], scaled[j][:, e, :], ALU.add).then_inc(sum_done, 1)

            pool.wait_ge(affine_in, 2 * LOADS)
            make_x1(0, 0, 0)
            make_x1(1, 1, 0)
            add_z(GALL - 2, GALL - 2, 0)
            start_sum(0, 0)
            make_x1(2, 0, 1)

            def phase3(p):
                for j in range(2):
                    T = 2 * p + j
                    if not (known(T) and T + 1 >= NT):
                        start_sum(T + 1, 1 - j)
                    if not (known(T) and T + 3 >= NT):
                        make_x1(T + 3, 1 - j, p + 1 + j)
                    if known(T) and T == 0:
                        add_z(GALL - 1, GALL - 1, 1)
                    if not (known(T) and T == NT - 1):
                        finish_sum(T, j, p)

            phase3(0)
            with pool.Fori(1, NT // 2 - 2) as p:
                phase3(p)
            phase3(NT // 2 - 2)
            phase3(NT // 2 - 1)

        @block.scalar
        def _(act):
            act.wait_ge(consts_set, 1)

            def take_std(n, j):
                act.wait_ge(var_done, n + 1)
                nc.scalar.activation(std[:, j, :], mv[:, j, :, 1], ACT.Sqrt, bias=eps[:, 0:1]).then_inc(std_done, 1)

            def high_parts(n, j, p, side, ready, bank, bias, halves=range(KC)):
                act.wait_ge(ready, n + 1)
                if not (known(p) and p == 0):
                    act.wait_ge(op_stored[side][j], STORES[side] * p)
                for m in halves:
                    nc.scalar.activation(parts[j][:, side, 0, m, :], ps[:, bank + m, :], ACT.Identity,
                                         bias=bias[:, m:m + 1]).then_inc(hi_done[side], 1)
                    if known(n) and n == B - 1:
                        act.wait_ge(lo_done[side], n)
                        act.wait_ge(mid_done[side], n)
                        nc.scalar.activation(rest[:, side, m, :], ps[:, bank + m, :], ACT.Identity,
                                             bias=bias[:, m:m + 1]).then_inc(last_copied[side], 1)

            def middle_part(n, j, side):
                act.wait_ge(rest_done[side], KC * (n + 1))
                nc.scalar.activation(parts[j][:, side, 1, :, :], rest[:, side, :, :], ACT.Copy).then_inc(mid_done[side], 1)

            def high_shift(G, i):
                act.wait_ge(maxT_ready, G + 1)
                if not (known(G) and G < 2):
                    act.wait_ge(sh_stored, LOADS * (G - 1))
                nc.scalar.activation(shift_parts[:, i, 0, :], maxT[:, i, :], ACT.Copy, scale=-1.0).then_inc(sh_hi, 1)
                nc.scalar.activation(shift[:, i, :], maxT[:, i, :], ACT.Copy, scale=-1.0).then_inc(shift_set, 1)

            def high_ctx(n, j, p):
                act.wait_ge(ctx_loaded[j], LOADS * (p + 1))
                if not (known(n) and n < 2):
                    act.wait_ge(v_ready, n - 1)
                nc.scalar.activation(ctx_hi[j], ctx_in[j], ACT.Copy).then_inc(ctx_high, 1)

            nc.scalar.activation(std[:, 0, 0:1], eps[:, 0:1], ACT.Copy).then_inc(std_done, 1)
            act.wait_ge(wk_in, LOADS)
            nc.scalar.activation(wk_hi, wk, ACT.Copy).then_inc(w_high, 1)
            high_ctx(0, 0, 0)
            take_std(0, 0)
            act.wait_ge(wv_in, LOADS)
            nc.scalar.activation(wv_hi, wv, ACT.Copy).then_inc(w_high, 1)
            act.wait_ge(wq_in, LOADS)
            nc.scalar.activation(wq_hi, wq, ACT.Copy).then_inc(w_high, 1)
            act.wait_ge(bias_k_in, LOADS)
            act.wait_ge(bias_q_in, LOADS)

            def phase1(p):
                for j in range(2):
                    n = 2 * p + j
                    last = known(n) and n == B - 1
                    if not last:
                        high_ctx(n + 1, 1 - j, p + j)
                    high_parts(n, j, p, 1, k_ready, 4, bias_k, (0,))
                    act.wait_ge(xT_ready, n + 1)
                    nc.scalar.activation(xnT_hi, ps[:, 0:KC, :], ACT.Copy).then_inc(xnT_high, 1)
                    high_parts(n, j, p, 1, k_ready, 4, bias_k, (1,))
                    if not last:
                        take_std(n + 1, 1 - j)
                    if not (known(n) and n == 0):
                        middle_part(n - 1, 1 - j, 0)
                    middle_part(n, j, 1)
                    act.wait_ge(xn_done, n + 1)
                    nc.scalar.activation(normed[:, bass.ds(TT * n, TT), :], xn[j], ACT.Copy).then_inc(xn_kept, 1)
                    if last:
                        act.wait_ge(v_ready, B)
                        nc.scalar.activation(v_all[:, n, :, :], ps[:, 6:8, :].rearrange("p b (t d) -> p (b t) d", d=D), ACT.Copy).then_inc(v_done, 1)
                    high_parts(n, j, p, 0, q_ready, 4 if last else 2, bias_q)

            phase1(0)
            with act.Fori(1, B // 2 - 1) as p:
                phase1(p)
            phase1(B // 2 - 1)
            high_shift(0, 0)
            middle_part(B - 1, 1, 0)

            def e_take_std(r, n=2):
                act.wait_ge(e_var, r + 1)
                if not (known(r) and r == 0):
                    act.wait_ge(e_rstd, r)
                nc.scalar.activation(std[:, 0, 0:n], mv[:, 0, 0:n, 1], ACT.Sqrt, bias=eps[:, 0:1]).then_inc(e_std, 1)

            def take_zT(G, i):
                act.wait_ge(pv_done, G + 1)
                if not (known(G) and G < 2):
                    act.wait_ge(zt_done, 2 * (G - 1))
                elif G == 0:
                    act.wait_ge(xn_kept, B)
                nc.scalar.activation(zT[:, i, :], ps[:, ZT_BANK, :], ACT.Copy).then_inc(zT_done, 1)

            def phase2(b):
                for g in range(NG):
                    G = NG * b + g
                    for h in range(HG):
                        for kt in range(TT):
                            n = HG * TT * G + TT * h + kt
                            act.wait_ge(st_ready, n + 1)
                            if h == 0 and kt == 0 and known(G) and G == 1:
                                for side in range(2):
                                    for j in range(2):
                                        act.wait_ge(op_stored[side][j], STORES[side] * (B // 2))
                            if h == 0 and kt == 0 and not (known(G) and G < 2):
                                act.wait_ge(pv_done, G - 1)
                            nc.scalar.activation(probs[:, g % 2, h, kt, :], st_bank(TT * (HG * g + h) + kt), ACT.Exp).then_inc(exp_done, 1)
                            soon = known(G) and G in (0, GALL - 2)
                            if h == (0 if soon else 1) and kt == 0 and not (known(G) and G + 1 >= GALL):
                                high_shift(G + 1, (g + 1) % 2)
                            if h == 1 and kt == TT - 1 and known(G) and G == GALL - 3:
                                e_take_std(0, EARLY)
                    if not (known(G) and (G < 1 or G >= GALL - 2)):
                        take_zT(G - 1, (g + 1) % 2)

            for_batches(act, phase2)

            def take_xfT(T, j):
                act.wait_ge(xfT_ready, T + 1)
                if not (known(T) and T < 2):
                    act.wait_ge(expert_ready, (E // 2) * (T - 1))
                nc.scalar.activation(xfT[j], ps[:, 4, 0:D].rearrange("p (c s) -> p c s", c=KC), ACT.Copy).then_inc(xfT_whole, 1)
                act.wait_ge(xfT_whole, T + 1)
                nc.scalar.activation(xfT_hi[:, j, :, :], xfT[j], ACT.Copy).then_inc(xfT_high, 1)

            def scale_last(T, j):
                act.wait_ge(best_done, 4 * (T + 1))
                if not (known(T) and T < 2):
                    act.wait_ge(sum_done, 3 * (T - 1))
                act.wait_ge(expert_ready, (E // 2) * (T + 1))
                for e in range(2):
                    nc.scalar.activation(scaled[j][:, e, :], ps[:, E // 2 - 1, e * D:(e + 1) * D], ACT.Copy,
                                         scale=chosen[j][:, MIX + e:MIX + e + 1]).then_inc(scaled_done, 1)

            e_take_std(1)
            take_xfT(0, 0)
            take_zT(GALL - 1, 1)

            def phase3(p):
                for j in range(2):
                    T = 2 * p + j
                    if not (known(T) and T + 1 >= NT):
                        e_take_std(T + 2)
                        take_xfT(T + 1, 1 - j)
                    if not (known(T) and T == NT - 1):
                        scale_last(T, j)

            phase3(0)
            with act.Fori(1, NT // 2 - 1) as p:
                phase3(p)
            phase3(NT // 2 - 1)

        @block.vector
        def _(dve):
            def batch_stats(n, j, p):
                dve.wait_ge(x_loaded[j], LOADS * (p + 1))
                for t in range(TT):
                    nc.vector.bn_stats(bn[:, j, t, :], x_in[j][:, t, :]).then_inc(stats_step, 1)
                dve.wait_ge(stats_step, TT * (n + 1))
                carry_wait_dve()
                for t in range(TT):
                    ins = nc.vector.bn_aggr(mv[:, j, t, :], bn[:, j, t, :])
                ins.then_inc(var_done, 1)

            def norm_batch(n, j):
                dve.wait_ge(std_done, n + 2)
                nc.vector.reciprocal(rstd[:, j, :], std[:, j, :]).then_inc(rstd_done, 1)
                dve.wait_ge(rstd_done, n + 1)
                dve.wait_ge(var_done, n + 1)
                if not (known(n) and n < 2):
                    dve.wait_ge(xT_ready, n - 1)
                    dve.wait_ge(xn_kept, n - 1)
                for t in range(TT):
                    ins = nc.vector.tensor_scalar(xn[j][:, t, :], x_in[j][:, t, :], mv[:, j, t, 0:1], rstd[:, j, t:t + 1],
                                                  ALU.subtract, ALU.mult)
                ins.then_inc(xn_done, 1)

            def take_rest(n, j, side, bank, bias, halves=range(KC)):
                if not (known(n) and n == 0):
                    dve.wait_ge(lo_done[side], n)
                    dve.wait_ge(mid_done[side], n)
                for m in halves:
                    dve.wait_ge(hi_done[side], KC * n + m + 1)
                    nc.vector.scalar_tensor_tensor(rest[:, side, m, :], ps[:, bank + m, :], bias[:, m:m + 1],
                                                   parts[j][:, side, 0, m, :], ALU.add, ALU.subtract).then_inc(rest_done[side], 1)

            def row_maxima(G, i, unit):
                dve.wait_ge(scores_ready, 2 * HG * G + unit + 1)
                nc.vector.reduce_max(row_max[:, i, 2 * unit:2 * unit + 2], mx_bank(G, unit), AX_X).then_inc(max_done, 1)

            def transpose_max(G, i):
                dve.wait_ge(max_done, 2 * HG * (G + 1))
                if not (known(G) and G < 2):
                    dve.wait_ge(shift_set, G - 1)
                nc.vector.transpose(maxT[:, i, :], row_max[:, i, :]).then_inc(maxT_ready, 1)

            def low_weight(i, w, w_hi, w_lo):
                dve.wait_ge(w_high, i + 1)
                nc.vector.tensor_tensor(w_lo, w, w_hi.bitcast(F32), ALU.subtract).then_inc(w_low, 1)

            low_weight(0, wk, wk_hi, wk_lo)
            dve.wait_ge(ctx_loaded[0], LOADS)
            dve.wait_ge(ctx_high, 1)
            nc.vector.tensor_tensor(ctx_lo[0], ctx_in[0], ctx_hi[0].bitcast(F32), ALU.subtract).then_inc(ctx_low, 1)
            batch_stats(0, 0, 0)
            norm_batch(0, 0)
            low_weight(1, wv, wv_hi, wv_lo)
            low_weight(2, wq, wq_hi, wq_lo)
            dve.wait_ge(bias_k_in, LOADS)
            dve.wait_ge(bias_v_in, LOADS)
            dve.wait_ge(bias_q_in, LOADS)

            def phase1(p):
                for j in range(2):
                    n = 2 * p + j
                    last = known(n) and n == B - 1

                    def first_max(*units):
                        if last:
                            for unit in units:
                                row_maxima(0, 0, unit)
                    if last:
                        dve.wait_ge(consts_set, 4 + E)
                    else:
                        batch_stats(n + 1, 1 - j, p + j)
                    if not (known(n) and n == 0):
                        take_rest(n - 1, 1 - j, 0, 2, bias_q)
                    first_max(0)
                    if not last:
                        take_rest(n, j, 1, 4, bias_k, (0,))
                    dve.wait_ge(xT_ready, n + 1)
                    dve.wait_ge(xnT_high, n + 1)
                    nc.vector.tensor_tensor(xnT_lo, ps[:, 0:KC, :], xnT_hi.bitcast(F32), ALU.subtract).then_inc(xnT_low, 1)
                    if not last:
                        take_rest(n, j, 1, 4, bias_k, (1,))
                    first_max(1)
                    if not last:
                        norm_batch(n + 1, 1 - j)
                    if not last:
                        dve.wait_ge(v_ready, n + 1)
                        for i in range(2):
                            ins = nc.vector.tensor_tensor(v_all[:, n, 2 * i:2 * i + 2, :],
                                                          ps[:, 6 + i, :].rearrange("p (t d) -> p t d", t=2),
                                                          bias_v[:, :].rearrange("p (a d) -> p a d", a=1).broadcast_to([P, 2, D]), ALU.add)
                        ins.then_inc(v_done, 1)
                    first_max(*range(2, 2 * HG))

            phase1(0)
            with dve.Fori(1, B // 2 - 1) as p:
                phase1(p)
            phase1(B // 2 - 1)
            transpose_max(0, 0)

            def token_major(G, i, step):
                if step < 2:
                    if step == 0:
                        dve.wait_ge(zT_done, G + 1)
                        if not (known(G) and G < 2):
                            dve.wait_ge(z_done, G - 1)
                    half = slice(step * DH // 2, (step + 1) * DH // 2)
                    nc.vector.transpose(zt[:, i, half, :], zT[:, i, :].rearrange("p (a c) -> p c a", c=DH)[:, half]).then_inc(zt_done, 1)
                else:
                    dve.wait_ge(zt_done, 2 * (G + 1))
                    nc.vector.reciprocal(recip[:, i, :], zt[:, i, :, DH]).then_inc(recip_done, 1)

            def take_zT(G, i):
                dve.wait_ge(pv_done, G + 1)
                dve.wait_ge(zt_done, 2 * (G - 1))
                nc.vector.tensor_copy(zT[:, i, :], ps[:, ZT_BANK, :]).then_inc(zT_done, 1)

            def whole_token_major(G, i):
                for step in range(3):
                    token_major(G, i, step)

            for unit in range(2 * HG):
                row_maxima(1, 1, unit)
            transpose_max(1, 1)

            source = {0: lambda T, j: normed[:, T, :], 1: lambda T, j: x1[j]}

            def gather_stats(slots, count):
                dve.wait_ge(e_stats, count)
                carry_wait_dve()
                for i in slots:
                    ins = nc.vector.bn_aggr(mv[:, 0, i, :], bn[:, 0, i, :])
                ins.then_inc(e_var, 1)

            def invert_std(r, n):
                dve.wait_ge(e_std, r + 1)
                nc.vector.reciprocal(rstd[:, 0, 0:n], std[:, 0, 0:n]).then_inc(e_rstd, 1)

            def apply_norm(i, T, j, slot):
                if i == 0:
                    if not (known(T) and T < 2):
                        dve.wait_ge(x1_done, T - 1)
                elif not (known(T) and T < 2):
                    dve.wait_ge(even_set, T - 1)
                    dve.wait_ge(xfT_ready, T - 1)
                nc.vector.tensor_scalar((u, xf)[i][j], source[i](T, j), mv[:, 0, slot, 0:1], rstd[:, 0, slot:slot + 1],
                                        ALU.subtract, ALU.mult).then_inc((u_done, xf_done)[i], 1)

            def two_norms(r, a, b, between):
                todo = [(i, t) for i, t in ((0, a), (1, b)) if t is not None]
                dve.wait_ge(x1_done, b[0] + 1)
                for i, t in todo:
                    nc.vector.bn_stats(bn[:, 0, i, :], source[i](*t)).then_inc(e_stats, 1)
                between[0]()
                gather_stats([i for i, _ in todo], NT + r if a is None else 2 * r + 2)
                between[1]()
                invert_std(r, 2)
                dve.wait_ge(e_rstd, r + 1)
                dve.wait_ge(e_var, r + 1)
                for i, t in reversed(todo):
                    apply_norm(i, *t, i)

            def phase2(b):
                for g in range(NG):
                    G = NG * b + g
                    for unit in range(2 * HG):
                        if not (known(G) and G + 2 >= GALL):
                            row_maxima(G + 2, g % 2, unit)
                        if unit == 0 and not (known(G) and (G == 0 or G + 1 >= GALL)):
                            transpose_max(G + 1, (g + 1) % 2)
                        if 2 <= unit <= 4 and not (known(G) and G < 2):
                            token_major(G - 2, g % 2, unit - 2)
                    if known(G) and G == GALL - 4:
                        dve.wait_ge(y_done, EARLY)
                        for T in range(EARLY):
                            nc.vector.bn_stats(bn[:, 0, T, :], normed[:, T, :]).then_inc(e_stats, 1)
                        gather_stats(range(EARLY), EARLY)
                    if known(G) and G == GALL - 2:
                        dve.wait_ge(experts_in, LOADS)
                        nc.vector.tensor_copy(experts_hi[:, :, :], experts).then_inc(experts_cut, 1)
                        invert_std(0, EARLY)
                        dve.wait_ge(e_rstd, 1)
                        dve.wait_ge(st_ready, HG * TT * (GALL - 2))
                        apply_norm(0, 0, 0, 0)
                        apply_norm(0, 1, 1, 1)
                        take_zT(G - 1, (g + 1) % 2)

            for_batches(dve, phase2)
            dve.wait_ge(experts_cut, 1)
            dve.wait_ge(v_aug_done, GALL)
            nc.vector.tensor_tensor(experts_lo[:, :, :], experts, experts_hi[:, :, :].bitcast(F32), ALU.subtract).then_inc(experts_ready, 1)

            def choose(T, j, step):
                score = ps[:, 5, 0:E]
                if step == 0:
                    dve.wait_ge(gate_ready, T + 1)
                    nc.vector.reduce_max(best, score, AX_X).then_inc(best_done, 1)
                elif step == 1:
                    dve.wait_ge(best_done, 4 * T + 1)
                    nc.vector.scalar_tensor_tensor(tied, score, best, rank_weight[:, :], ALU.is_equal, ALU.mult).then_inc(best_done, 1)
                elif step == 2:
                    dve.wait_ge(best_done, 4 * T + 2)
                    nc.vector.reduce_max(first, tied, AX_X).then_inc(best_done, 1)
                else:
                    if not (known(T) and T < 2):
                        dve.wait_ge(scaled_done, 2 * (T - 1))
                    dve.wait_ge(best_done, 4 * T + 3)
                    nc.vector.tensor_scalar(chosen[j], rank_weight[:, :], first, None, ALU.is_equal).then_inc(best_done, 1)

            def mix(T, j, e):
                if e == 0:
                    dve.wait_ge(best_done, 4 * T + 4)
                    dve.wait_ge(even_set, T + 1)
                if e % 2 == 0:
                    dve.wait_ge(expert_ready, (E // 2) * T + e // 2 + 1)
                if e >= 2:
                    dve.wait_ge(mix_done, MIX * T + e - 1)
                out_e = ps[:, e // 2, (e % 2) * D:(e % 2 + 1) * D]
                if e == 1:
                    if not (known(T) and T < 2):
                        dve.wait_ge(sum_done, 3 * (T - 1))
                    nc.vector.tensor_scalar(odd[j], out_e, chosen[j][:, e:e + 1], None, ALU.mult).then_inc(mix_done, 1)
                else:
                    total = (even, odd)[e % 2][j]
                    nc.vector.scalar_tensor_tensor(total, out_e, chosen[j][:, e:e + 1], total, ALU.mult, ALU.add).then_inc(mix_done, 1)

            def low_xfT(T, j):
                dve.wait_ge(xfT_high, T + 1)
                if not (known(T) and T < 2):
                    dve.wait_ge(expert_ready, (E // 2) * (T - 1))
                nc.vector.tensor_tensor(xfT_lo[:, j, :, :], xfT[j],
                                        xfT_hi[:, j, :, :].bitcast(F32), ALU.subtract).then_inc(xfT_low, 1)

            apply_norm(0, 2, 0, 2)
            dve.wait_ge(x1_done, 1)
            nc.vector.bn_stats(bn[:, 0, 1, :], x1[0]).then_inc(e_stats, 1)
            gather_stats([1], EARLY + 1)
            take_zT(GALL - 2, 0)
            whole_token_major(GALL - 2, 0)
            invert_std(1, 2)
            dve.wait_ge(e_rstd, 2)
            dve.wait_ge(e_var, 2)
            apply_norm(1, 0, 0, 1)
            low_xfT(0, 0)
            dve.wait_ge(y_done, GALL - 4)

            def phase3(p):
                for j in range(2):
                    T = 2 * p + j

                    def early():
                        choose(T, j, 0)
                        choose(T, j, 1)

                    def middle():
                        choose(T, j, 2)
                        choose(T, j, 3)

                    def late():
                        mix(T, j, 0)
                        mix(T, j, 1)
                    if known(T) and T + 1 >= NT:
                        early(), middle(), late()
                        for e in range(2, E):
                            mix(T, j, e)
                        dve.wait_ge(mix_done, MIX * T + E)
                        dve.wait_ge(out_stored[j], LOADS * (NT // 2 - 1))
                        nc.vector.tensor_tensor(result[j], even[j], odd[j], ALU.add).then_inc(last_sum_done, 1)
                    else:
                        a = None if known(T) and T + 3 >= NT else (T + 3, 1 - j)
                        two_norms(T + 2, a, (T + 1, 1 - j), [early, middle])
                        late()
                        low_xfT(T + 1, 1 - j)
                        mix(T, j, 2)
                        mix(T, j, 3)
                        mix(T, j, 4)
                        mix(T, j, 5)
                    if known(T) and T == 0:
                        whole_token_major(GALL - 1, 1)

            phase3(0)
            dve.wait_ge(y_done, GALL)
            with dve.Fori(1, NT // 2 - 2) as p:
                phase3(p)
            phase3(NT // 2 - 2)
            phase3(NT // 2 - 1)

        @block.tensor
        def _(pe):
            def thirds(dst, pairs):
                for n, (l, r) in enumerate(pairs):
                    ins = nc.tensor.matmul(dst, l, r, start=(n == 0), stop=(n == len(pairs) - 1))
                return ins

            batch_of = {}

            def G_batch(G):
                return G // NG if known(G) else batch_of["b"]

            def G_pair(G):
                return G // 2 + 1 if known(G) else 2 * batch_of["b"] + batch_of["g"] // 2 + 1

            def score_unit(G, g, h, half):
                for qt in (2 * half, 2 * half + 1):
                    score(G, g, h, qt)

            def score(G, g, h, qt):
                unit = 2 * h + qt // 2
                if qt % 2 == 0:
                    if h == 0 and qt == 0:
                        b = G_batch(G)
                        pe.wait_ge(op_loaded[g], OP_LOADS * (b + 1))
                    if known(G) and G == 0:
                        if unit == 0:
                            pe.wait_ge(rest_done[0], KC * (B - 1))
                        elif unit == 2:
                            pe.wait_ge(xnT_low, B)
                        else:
                            pe.wait_ge(max_done, max(unit - 1, 1))
                    else:
                        pe.wait_ge(max_done, 2 * HG * G + unit - 1)
                hd = HG * g + h
                ins = nc.tensor.matmul(mx_bank(G, unit)[:, qt % 2, :], q_op[0:ROWS, hd, qt * P:(qt + 1) * P], k_op[0:ROWS, hd, :],
                                       start=True, stop=True)
                if qt % 2:
                    ins.then_inc(scores_ready, 1)

            def phase1(p):
                for j in range(2):
                    n = 2 * p + j
                    first = known(n) and n == 0
                    last = known(n) and n == B - 1

                    def first_max(*units):
                        if last:
                            for unit in units:
                                score_unit(0, 0, unit // 2, unit % 2)
                    if first:
                        pe.wait_ge(w_low, 1)
                        pe.wait_ge(w_high, 1)
                    pe.wait_ge(ctx_high, n + 1)
                    if not first:
                        pe.wait_ge(rest_done[1], KC * n)
                    for m in range(KC):
                        for c in range(KC):
                            for w in (wk_hi, wk_lo):
                                nc.tensor.matmul(ps[:, 4 + m, :], w[:, c, m * P:(m + 1) * P], ctx_hi[j][:, c, :],
                                                 start=(c == 0 and w is wk_hi), stop=False)
                    pe.wait_ge(ctx_low, n + 1)
                    for m in range(KC):
                        for c in range(KC):
                            ins = nc.tensor.matmul(ps[:, 4 + m, :], wk_hi[:, c, m * P:(m + 1) * P], ctx_lo[j][:, c, :],
                                                   start=False, stop=(c == KC - 1))
                    ins.then_inc(k_ready, 1)
                    first_max(0)
                    if first:
                        pe.wait_ge(identity_loaded, LOADS)
                    pe.wait_ge(xn_done, n + 1)
                    if not first:
                        pe.wait_ge(xnT_low, n)
                    for t in range(TT):
                        for c in range(KC):
                            ins = nc.tensor.transpose(ps[:, c, t * P:(t + 1) * P], xn[j][:, t, c * P:(c + 1) * P], identity[:, :])
                    ins.then_inc(xT_ready, 1)
                    if first:
                        pe.wait_ge(w_low, 2)
                        pe.wait_ge(w_high, 2)
                    else:
                        pe.wait_ge(v_done, n)
                    for t in range(TT):
                        rows = slice(t * P, (t + 1) * P)
                        ins = thirds(ps[:, 6 + t // 2, (t % 2) * D:(t % 2 + 1) * D], [(x[:, c, rows], w[:, c, :]) for c in range(KC) for x, w in (
                            (ctx_hi[j], wv_hi), (ctx_lo[j], wv_hi), (ctx_hi[j], wv_lo))])
                    ins.then_inc(v_ready, 1)
                    first_max(1, 2, 3)
                    if first:
                        pe.wait_ge(w_low, 3)
                        pe.wait_ge(w_high, 3)
                    pe.wait_ge(xnT_high, n + 1)
                    pe.wait_ge(xnT_low, n + 1)
                    if last:
                        pe.wait_ge(last_copied[1], KC)
                    elif not first:
                        pe.wait_ge(rest_done[0], KC * n)
                    for m in range(KC):
                        cols = slice(m * P, (m + 1) * P)
                        ins = thirds(ps[:, (4 if last else 2) + m, :], [(w[:, c, cols], t[:, c, :]) for c in range(KC) for w, t in (
                            (wq_hi, xnT_hi), (wq_lo, xnT_hi), (wq_hi, xnT_lo))])
                    ins.then_inc(q_ready, 1)
                    first_max(*range(4, 2 * HG))

            phase1(0)
            with pe.Fori(1, B // 2 - 1) as p:
                phase1(p)
            phase1(B // 2 - 1)
            pe.wait_ge(last_copied[0], KC)
            pe.wait_ge(v_done, B)
            pe.wait_ge(xnT_low, B)
            pe.wait_ge(ones_set, NG)

            def shifted(G, g, h, kt):
                n = TT * (HG * g + h) + kt
                if h == 0 and kt == 0:
                    pe.wait_ge(sh_loaded[g % 2], 3 * LOADS * G_pair(G))
                if not (known(G) and TT * HG * G + TT * h + kt < 3):
                    pe.wait_ge(exp_done, ST_BATCH * G_batch(G) + st_before(n))
                hd = HG * g + h
                nc.tensor.matmul(st_bank(n), k_op[0:SROWS, hd, kt * P:(kt + 1) * P], q_op[0:SROWS, hd, :],
                                 start=True, stop=True).then_inc(st_ready, 1)

            def attend(G, i, kt):
                if kt == 0:
                    pe.wait_ge(v_aug_done, G + 1)
                    if not (known(G) and G == 0):
                        pe.wait_ge(zT_done, G)
                pe.wait_ge(exp_done, HG * TT * G + (HG - 1) * TT + kt + 1)
                for h in range(HG):
                    ins = nc.tensor.matmul(ps[2 * DH * h:2 * DH * (h + 1), ZT_BANK, :], v_aug[:, i, kt, h, :],
                                           probs[:, i, h, kt, :], start=(kt == 0), stop=(kt == TT - 1),
                                           tile_position=(0, 2 * DH * h))
                if kt == TT - 1:
                    ins.then_inc(pv_done, 1)

            for h in range(HG):
                for half in range(2):
                    score_unit(1, 1, h, half)

            def phase2(b):
                for g in range(NG):
                    G = NG * b + g

                    def mx(h, half, second):
                        if not (known(G) and G + 2 >= GALL):
                            batch_of["b"] = b + (g + 2) // NG
                            score(G + 2, (g + 2) % NG, h, 2 * half + second)

                    def st(h, kt):
                        batch_of["b"], batch_of["g"] = b, g
                        shifted(G, g, h, kt)

                    for h in range(HG):
                        st(h, 0)
                        mx(h, 0, 0)
                        st(h, 1)
                        mx(h, 0, 1)
                        st(h, 2)
                        if not (known(G) and G == 0):
                            attend(G - 1, (g + 1) % 2, h)
                        mx(h, 1, 0)
                        st(h, 3)
                        mx(h, 1, 1)

            for_batches(pe, phase2)

            def transpose_xf(T, j):
                pe.wait_ge(xf_done, T + 1)
                if not (known(T) and T == 0):
                    pe.wait_ge(xfT_whole, T)
                for c in range(KC):
                    ins = nc.tensor.transpose(ps[:, 4, c * P:(c + 1) * P], xf[j][:, c * P:(c + 1) * P], identity[:, :])
                ins.then_inc(xfT_ready, 1)

            def halves(T, j, dst, cols):
                passes = [(l, r, c) for c in range(KC) for l, r in ((xfT_hi, experts_hi), (xfT_lo, experts_hi), (xfT_hi, experts_lo))]
                for n, (l, r, c) in enumerate(passes):
                    ins = nc.tensor.matmul(dst, l[:, j, c, :], r[:, c, cols], start=(n == 0), stop=(n == len(passes) - 1))
                return ins

            def gates(T, j):
                pe.wait_ge(xfT_whole, T + 1)
                if not (known(T) and T == 0):
                    pe.wait_ge(best_done, 4 * T)
                for c in range(KC):
                    ins = nc.tensor.matmul(ps[:, 5, 0:E], xfT[j][:, c, :], gate[:, c, :], start=(c == 0), stop=(c == KC - 1))
                ins.then_inc(gate_ready, 1)

            def expert_pair(T, j, i):
                if i == 0:
                    pe.wait_ge(xfT_high, T + 1)
                    pe.wait_ge(xfT_low, T + 1)
                if not (known(T) and T == 0):
                    if i < MIX // 2:
                        pe.wait_ge(mix_done, MIX * (T - 1) + 2 * i + 2)
                    else:
                        pe.wait_ge(scaled_done, 2 * T)
                halves(T, j, ps[:, i, :], slice(2 * D * i, 2 * D * (i + 1))).then_inc(expert_ready, 1)

            for kt in range(TT):
                if kt == TT - 1:
                    pe.wait_ge(max_done, 2 * HG * GALL)
                    transpose_xf(0, 0)
                attend(GALL - 1, 1, kt)
            pe.wait_ge(exp_done, HG * TT * GALL)
            pe.wait_ge(gate_in, LOADS)
            pe.wait_ge(experts_ready, 1)
            pe.wait_ge(experts_cut, 1)
            gates(0, 0)

            def phase3(p):
                for j in range(2):
                    T = 2 * p + j
                    more = not (known(T) and T + 1 >= NT)
                    for i in range(E // 2):
                        expert_pair(T, j, i)
                        if i == 1 and more:
                            transpose_xf(T + 1, 1 - j)
                    if more:
                        gates(T + 1, 1 - j)

            phase3(0)
            with pe.Fori(1, NT // 2 - 1) as p:
                phase3(p)
            phase3(NT // 2 - 1)


def kernel(x, ctx_1024, L0_xattn_Wq, L0_xattn_bq, L0_xattn_Wk, L0_xattn_bk, L0_xattn_Wv, L0_xattn_bv,
           L0_xattn_gamma, L0_xattn_beta, L0_ffn_gate_w, L0_ffn_expert_w):
    import numpy as np
    import concourse.bacc as bacc
    from concourse.bass_utils import run_bass_kernel_spmd

    D = x.shape[-1]
    dh = D // H
    half = P // dh
    order = np.array([(m * half + p % half) * dh + p // half for m in range(D // P) for p in range(P)])
    c = np.ascontiguousarray
    arrays = {
        "x": c(x),
        "ctxT": c(np.transpose(np.asarray(ctx_1024), (0, 2, 1))),
        "WqT": c(np.asarray(L0_xattn_Wq)[order].T),
        "bq": c(np.asarray(L0_xattn_bq)[order].reshape(D // P, P).T),
        "WkT": c(np.asarray(L0_xattn_Wk)[order].T),
        "bk": c(np.asarray(L0_xattn_bk)[order].reshape(D // P, P).T),
        "WvT": c(np.asarray(L0_xattn_Wv).T),
        "bv": c(L0_xattn_bv),
        "gamma": c(L0_xattn_gamma),
        "beta": c(L0_xattn_beta),
        "gateT": c(np.asarray(L0_ffn_gate_w).T),
        "expertT": c(np.transpose(np.asarray(L0_ffn_expert_w), (2, 0, 1)).reshape(D, -1)),
        "identity_in": np.eye(P, dtype=np.float32),
    }
    nc = bacc.Bacc("TRN2", target_bir_lowering=False, num_devices=1)
    args = [nc.dram_tensor(f"in_{k}", a.shape, mybir.dt.from_np(a.dtype), kind="ExternalInput").ap() for k, a in arrays.items()]
    out = nc.dram_tensor("out_0", x.shape, F32, kind="ExternalOutput").ap()
    xattn_ffn_kernel(nc, *args, out)
    r = run_bass_kernel_spmd(nc, [{f"in_{k}": a for k, a in arrays.items()}], core_ids=[0])
    return r.results[0]["out_0"]
```
